# Optimizing a Trainium2 kernel written in Bass

```python
import numpy as np
import jax
import jax.numpy as jnp

def _softmax(x, axis=-1):
    return jax.nn.softmax(x, axis=axis)

def _gelu(x):
    return jax.nn.gelu(x, approximate=True)

def _silu(x):
    return jax.nn.silu(x)

def _sigmoid(x):
    return jax.nn.sigmoid(x)

def _layernorm(x, axis=-1, eps=1e-05):
    m = jnp.mean(x, axis=axis, keepdims=True)
    v = jnp.var(x, axis=axis, keepdims=True)
    return (x - m) / jnp.sqrt(v + eps)

def _scatter_add(tgt, idx, src, axis=0):
    return tgt.at[idx].add(src)

def _segment_sum(src, seg, n):
    return jax.ops.segment_sum(src, seg, n)
kernel_name = 'mk_xattn_ffn_d2_seqx_r4_57f8b8'

def setup_inputs(seed: int=0):
    np.random.seed(seed)
    _w = jnp.asarray

    def _rec_inputs():
        import jax
        import jax.numpy as jnp
        _rk = jax.random.key(seed)
        x = -0.0002928 + 1 * jax.random.normal(jax.random.fold_in(_rk, 1), (2, 1024, 256), jnp.float32)
        _lenS = 1024 - jax.random.randint(jax.random.fold_in(_rk, 7), (2,), 0, max(1, 1024 // 4) + 1, jnp.int32)
        _lenS2 = 77 - jax.random.randint(jax.random.fold_in(_rk, 8), (2,), 0, max(1, 77 // 4) + 1, jnp.int32)
        _ctx_768P = jax.random.normal(jax.random.fold_in(_rk, 11), (2, 16, 192), jnp.float32)
        _ctx_768c = jax.random.dirichlet(jax.random.fold_in(_rk, 511), 0.3 * jnp.ones((16,), jnp.float32), (2, 77))
        _ctx_768t = jnp.einsum('bsk,bkd->bsd', _ctx_768c, _ctx_768P)
        _ctx_768t = _ctx_768t * jax.lax.rsqrt(jnp.mean(jnp.square(_ctx_768t)) + 1e-12) * 0.953939
        ctx_768 = -8.43904e-05 + 0.999875 * (_ctx_768t + 0.3 * jax.random.normal(jax.random.fold_in(_rk, 611), (2, 77, 192), jnp.float32))
        _validS = jnp.arange(1024)[None, :] < _lenS[:, None]
        _validS2 = jnp.arange(77)[None, :] < _lenS2[:, None]
        _causal = jnp.tril(jnp.ones((1024, 1024), dtype=bool))
        mask_BxS2_bk0 = jnp.logical_not(jnp.broadcast_to(_validS2[:, :], (2, 77)))
        return (x, ctx_768, mask_BxS2_bk0)
    x, ctx_768, mask_BxS2_bk0 = _rec_inputs()

    def _L0_xattn_setup():
        import jax, jax.numpy as jnp
        import numpy as np
        LATENT_CH = 256
        INPUT_CH = 192
        QK_CH = 256
        V_CH = 256
        OUT_CH = 256
        NHEADS = 8
        EPS = 1e-05

        def layer_norm(x, gamma, beta):
            mu = jnp.mean(x, axis=-1, keepdims=True)
            var = jnp.var(x, axis=-1, keepdims=True)
            return (x - mu) * jax.lax.rsqrt(var + EPS) * gamma + beta
        key = jax.random.key(seed)
        ks = jax.random.split(key, 6)
        B, Lq, Lkv = (8, 128, 4096)
        latent_q = jax.random.normal(ks[0], (B, Lq, LATENT_CH), dtype=jnp.float32)
        input_kv = jax.random.normal(ks[1], (B, Lkv, INPUT_CH), dtype=jnp.float32)
        W_Q = jax.random.normal(ks[2], (LATENT_CH, QK_CH), dtype=jnp.float32) / np.sqrt(LATENT_CH)
        W_K = jax.random.normal(ks[3], (INPUT_CH, QK_CH), dtype=jnp.float32) / np.sqrt(INPUT_CH)
        W_V = jax.random.normal(ks[4], (INPUT_CH, V_CH), dtype=jnp.float32) / np.sqrt(INPUT_CH)
        W_O = jax.random.normal(ks[5], (V_CH, OUT_CH), dtype=jnp.float32) / np.sqrt(V_CH)
        ln_lat_g = jnp.ones((LATENT_CH,), jnp.float32)
        ln_lat_b = jnp.zeros((LATENT_CH,), jnp.float32)
        ln_in_g = jnp.ones((INPUT_CH,), jnp.float32)
        ln_in_b = jnp.zeros((INPUT_CH,), jnp.float32)
        return dict(latent_q=latent_q, input_kv=input_kv, W_Q=W_Q, W_K=W_K, W_V=W_V, W_O=W_O, ln_lat_g=ln_lat_g, ln_lat_b=ln_lat_b, ln_in_g=ln_in_g, ln_in_b=ln_in_b)
    _L0_xattn_all = _L0_xattn_setup()
    _L0_xattn_in = {k: v for k, v in _L0_xattn_all.items() if k in ('W_Q', 'W_K', 'W_V', 'W_O', 'ln_lat_g', 'ln_lat_b', 'ln_in_g', 'ln_in_b')}
    del _L0_xattn_all

    def _L0_ffn_setup():
        import jax, jax.numpy as jnp
        import numpy as np
        E, K = (8, 4)
        B, S, D = (4, 256, 256)
        H = D * 2 * 4 // 3

        def _swiglu(u, w1, w2, w3):
            h = jnp.einsum('...d,hd->...h', u, w1)
            v = jnp.einsum('...d,hd->...h', u, w2)
            return jnp.einsum('...h,dh->...d', jax.nn.sigmoid(h) * h * v, w3)
        key = jax.random.key(seed)
        ks = jax.random.split(key, 9)
        std = 0.02
        return {'x': jax.random.normal(ks[0], (B, S, D), jnp.float32), 'Wg': jax.random.normal(ks[1], (E, D), jnp.float32) * std, 'routing_bias': jnp.zeros((E,), jnp.float32), 'W1': jax.random.normal(ks[2], (E, H, D), jnp.float32) * std, 'W2': jax.random.normal(ks[3], (E, H, D), jnp.float32) * std, 'W3': jax.random.normal(ks[4], (E, D, H), jnp.float32) * std, 'Ws1': jax.random.normal(ks[5], (H, D), jnp.float32) * std, 'Ws2': jax.random.normal(ks[6], (H, D), jnp.float32) * std, 'Ws3': jax.random.normal(ks[7], (D, H), jnp.float32) * std}
    _L0_ffn_all = _L0_ffn_setup()
    _L0_ffn_in = {k: v for k, v in _L0_ffn_all.items() if k in ('Wg', 'routing_bias', 'W1', 'W2', 'W3', 'Ws1', 'Ws2', 'Ws3')}
    del _L0_ffn_all

    def _L1_xattn_setup():
        import jax, jax.numpy as jnp
        import numpy as np
        DIM_IN, DIM_LAT, DIM_HEAD = (192, 256, 64)
        INNER = max(DIM_LAT, DIM_IN)
        HEADS = INNER // DIM_HEAD
        SCALE = DIM_HEAD ** (-0.5)
        RMS_EPS = 1e-08
        LN_EPS = 1e-05

        def layernorm(x, g, b):
            mu = jnp.mean(x, axis=-1, keepdims=True)
            var = jnp.mean((x - mu) ** 2, axis=-1, keepdims=True)
            return (x - mu) * jax.lax.rsqrt(var + LN_EPS) * g + b

        def rmsnorm(x, gamma):
            norm = jnp.sqrt(jnp.sum(x * x, axis=-1, keepdims=True)) * x.shape[-1] ** (-0.5)
            return x / jnp.maximum(norm, RMS_EPS) * gamma
        key = jax.random.key(seed)
        ks = jax.random.split(key, 12)
        b, n, m = (4, 1024, 128)
        x = jax.random.normal(ks[0], (b, n, DIM_IN), jnp.float32)
        latents = jax.random.normal(ks[1], (b, m, DIM_LAT), jnp.float32)
        mask = jax.random.randint(ks[2], (b, n), 0, 2).astype(bool)
        s = lambda k, sh, fan: jax.random.normal(k, sh, jnp.float32) * fan ** (-0.5)
        return {'x': x, 'latents': latents, 'mask': mask, 'ln_x_g': jnp.ones((DIM_IN,), jnp.float32), 'ln_x_b': jnp.zeros((DIM_IN,), jnp.float32), 'ln_l_g': jnp.ones((DIM_LAT,), jnp.float32), 'ln_l_b': jnp.zeros((DIM_LAT,), jnp.float32), 'qn_g': jnp.ones((DIM_HEAD,), jnp.float32), 'kn_g': jnp.ones((DIM_HEAD,), jnp.float32), 'Wq': s(ks[3], (INNER, DIM_LAT), DIM_LAT), 'Wkv': s(ks[4], (2 * INNER, DIM_IN), DIM_IN), 'Wlkv': s(ks[5], (2 * INNER, DIM_LAT), DIM_LAT), 'Wo': s(ks[6], (DIM_LAT, INNER), INNER), 'bo': jnp.zeros((DIM_LAT,), jnp.float32)}
    _L1_xattn_all = _L1_xattn_setup()
    _L1_xattn_in = {k: v for k, v in _L1_xattn_all.items() if k in ('ln_x_g', 'ln_x_b', 'ln_l_g', 'ln_l_b', 'qn_g', 'kn_g', 'Wq', 'Wkv', 'Wlkv', 'Wo', 'bo')}
    del _L1_xattn_all

    def _L1_ffn_setup():
        import jax, jax.numpy as jnp
        import numpy as np
        from jax import lax
        D = 256
        H = 1024
        E = 8
        TOPK = 2
        key = jax.random.key(seed)
        ks = jax.random.split(key, 7)
        s = 0.02
        return {'x': jax.random.normal(ks[0], (2, 512, D), dtype=jnp.float32), 'W1': jax.random.normal(ks[1], (E, D, H), dtype=jnp.float32) * s, 'b1': jnp.zeros((E, H), dtype=jnp.float32), 'W2': jax.random.normal(ks[2], (E, H, D), dtype=jnp.float32) * s, 'b2': jnp.zeros((E, D), dtype=jnp.float32), 'Wr': jax.random.normal(ks[3], (D, E), dtype=jnp.float32) * s, 'br': jnp.zeros((E,), dtype=jnp.float32)}
    _L1_ffn_all = _L1_ffn_setup()
    _L1_ffn_in = {k: v for k, v in _L1_ffn_all.items() if k in ('W1', 'b1', 'W2', 'b2', 'Wr', 'br')}
    del _L1_ffn_all
    return {'x': x, 'ctx_768': ctx_768, 'mask_BxS2_bk0': mask_BxS2_bk0, 'L0_xattn_W_Q': _L0_xattn_in['W_Q'], 'L0_xattn_W_K': _L0_xattn_in['W_K'], 'L0_xattn_W_V': _L0_xattn_in['W_V'], 'L0_xattn_W_O': _L0_xattn_in['W_O'], 'L0_xattn_ln_lat_g': _L0_xattn_in['ln_lat_g'], 'L0_xattn_ln_lat_b': _L0_xattn_in['ln_lat_b'], 'L0_xattn_ln_in_g': _L0_xattn_in['ln_in_g'], 'L0_xattn_ln_in_b': _L0_xattn_in['ln_in_b'], 'L0_ffn_Wg': _L0_ffn_in['Wg'], 'L0_ffn_routing_bias': _L0_ffn_in['routing_bias'], 'L0_ffn_W1': _L0_ffn_in['W1'], 'L0_ffn_W2': _L0_ffn_in['W2'], 'L0_ffn_W3': _L0_ffn_in['W3'], 'L0_ffn_Ws1': _L0_ffn_in['Ws1'], 'L0_ffn_Ws2': _L0_ffn_in['Ws2'], 'L0_ffn_Ws3': _L0_ffn_in['Ws3'], 'L1_xattn_ln_x_g': _L1_xattn_in['ln_x_g'], 'L1_xattn_ln_x_b': _L1_xattn_in['ln_x_b'], 'L1_xattn_ln_l_g': _L1_xattn_in['ln_l_g'], 'L1_xattn_ln_l_b': _L1_xattn_in['ln_l_b'], 'L1_xattn_qn_g': _L1_xattn_in['qn_g'], 'L1_xattn_kn_g': _L1_xattn_in['kn_g'], 'L1_xattn_Wq': _L1_xattn_in['Wq'], 'L1_xattn_Wkv': _L1_xattn_in['Wkv'], 'L1_xattn_Wlkv': _L1_xattn_in['Wlkv'], 'L1_xattn_Wo': _L1_xattn_in['Wo'], 'L1_xattn_bo': _L1_xattn_in['bo'], 'L1_ffn_W1': _L1_ffn_in['W1'], 'L1_ffn_b1': _L1_ffn_in['b1'], 'L1_ffn_W2': _L1_ffn_in['W2'], 'L1_ffn_b2': _L1_ffn_in['b2'], 'L1_ffn_Wr': _L1_ffn_in['Wr'], 'L1_ffn_br': _L1_ffn_in['br']}

def reference(x, ctx_768, mask_BxS2_bk0, L0_xattn_W_Q, L0_xattn_W_K, L0_xattn_W_V, L0_xattn_W_O, L0_xattn_ln_lat_g, L0_xattn_ln_lat_b, L0_xattn_ln_in_g, L0_xattn_ln_in_b, L0_ffn_Wg, L0_ffn_routing_bias, L0_ffn_W1, L0_ffn_W2, L0_ffn_W3, L0_ffn_Ws1, L0_ffn_Ws2, L0_ffn_Ws3, L1_xattn_ln_x_g, L1_xattn_ln_x_b, L1_xattn_ln_l_g, L1_xattn_ln_l_b, L1_xattn_qn_g, L1_xattn_kn_g, L1_xattn_Wq, L1_xattn_Wkv, L1_xattn_Wlkv, L1_xattn_Wo, L1_xattn_bo, L1_ffn_W1, L1_ffn_b1, L1_ffn_W2, L1_ffn_b2, L1_ffn_Wr, L1_ffn_br):
    import jax
    import jax.numpy as jnp

    def _L0_xattn_ref(latent_q, input_kv, W_Q, W_K, W_V, W_O, ln_lat_g, ln_lat_b, ln_in_g, ln_in_b):
        import jax, jax.numpy as jnp
        import numpy as np
        LATENT_CH = 256
        INPUT_CH = 192
        QK_CH = 256
        V_CH = 256
        OUT_CH = 256
        NHEADS = 8
        EPS = 1e-05

        def layer_norm(x, gamma, beta):
            mu = jnp.mean(x, axis=-1, keepdims=True)
            var = jnp.var(x, axis=-1, keepdims=True)
            return (x - mu) * jax.lax.rsqrt(var + EPS) * gamma + beta
        B, Lq, _ = latent_q.shape
        _, Lkv, _ = input_kv.shape
        H = NHEADS
        dqk = QK_CH // H
        dv = V_CH // H
        lat = layer_norm(latent_q, ln_lat_g, ln_lat_b)
        inp = layer_norm(input_kv, ln_in_g, ln_in_b)
        Q = (lat @ W_Q).reshape(B, Lq, H, dqk)
        K = (inp @ W_K).reshape(B, Lkv, H, dqk)
        V = (inp @ W_V).reshape(B, Lkv, H, dv)
        scale = 1.0 / np.sqrt(dqk).astype(np.float32)
        attn = jnp.einsum('bqhd,bkhd->bhqk', Q, K) * scale
        attn = jax.nn.softmax(attn, axis=-1)
        out = jnp.einsum('bhqk,bkhd->bqhd', attn, V).reshape(B, Lq, V_CH)
        return out @ W_O

    def _L0_ffn_ref(x, Wg, routing_bias, W1, W2, W3, Ws1, Ws2, Ws3):
        import jax, jax.numpy as jnp
        import numpy as np
        E, K = (8, 4)
        B, S, D = (4, 256, 256)
        H = D * 2 * 4 // 3

        def _swiglu(u, w1, w2, w3):
            h = jnp.einsum('...d,hd->...h', u, w1)
            v = jnp.einsum('...d,hd->...h', u, w2)
            return jnp.einsum('...h,dh->...d', jax.nn.sigmoid(h) * h * v, w3)
        gate = jnp.einsum('bsd,ed->bse', x, Wg) + routing_bias
        _, top_idx = jax.lax.top_k(gate, K)
        mask = jax.nn.one_hot(top_idx, E, dtype=gate.dtype).sum(-2)
        masked_gate = jnp.where(mask > 0, gate, -jnp.inf)
        probs = jax.nn.softmax(masked_gate, axis=-1)
        weights = probs * mask
        out = _swiglu(x, Ws1, Ws2, Ws3)
        h1 = jnp.einsum('bsd,ehd->ebsh', x, W1)
        h2 = jnp.einsum('bsd,ehd->ebsh', x, W2)
        eo = jnp.einsum('ebsh,edh->ebsd', jax.nn.sigmoid(h1) * h1 * h2, W3)
        out = out + jnp.einsum('ebsd,bse->bsd', eo, weights)
        return out

    def _L1_xattn_ref(x, latents, mask, ln_x_g, ln_x_b, ln_l_g, ln_l_b, qn_g, kn_g, Wq, Wkv, Wlkv, Wo, bo):
        import jax, jax.numpy as jnp
        import numpy as np
        DIM_IN, DIM_LAT, DIM_HEAD = (192, 256, 64)
        INNER = max(DIM_LAT, DIM_IN)
        HEADS = INNER // DIM_HEAD
        SCALE = DIM_HEAD ** (-0.5)
        RMS_EPS = 1e-08
        LN_EPS = 1e-05

        def layernorm(x, g, b):
            mu = jnp.mean(x, axis=-1, keepdims=True)
            var = jnp.mean((x - mu) ** 2, axis=-1, keepdims=True)
            return (x - mu) * jax.lax.rsqrt(var + LN_EPS) * g + b

        def rmsnorm(x, gamma):
            norm = jnp.sqrt(jnp.sum(x * x, axis=-1, keepdims=True)) * x.shape[-1] ** (-0.5)
            return x / jnp.maximum(norm, RMS_EPS) * gamma
        b, n, _ = x.shape
        m = latents.shape[1]
        xn = layernorm(x, ln_x_g, ln_x_b)
        ln = layernorm(latents, ln_l_g, ln_l_b)
        q = ln @ Wq.T
        kv = jnp.concatenate([xn @ Wkv.T, ln @ Wlkv.T], axis=1)
        k, v = (kv[..., :INNER], kv[..., INNER:])
        split_heads = lambda t: t.reshape(t.shape[0], t.shape[1], HEADS, DIM_HEAD).transpose(0, 2, 1, 3)
        q, k, v = (split_heads(q), split_heads(k), split_heads(v))
        qn = rmsnorm(q, qn_g) * SCALE
        kn = rmsnorm(k, kn_g)
        attn = jnp.einsum('bhid,bhjd->bhij', qn, kn)
        full_mask = jnp.pad(mask, ((0, 0), (0, m)), constant_values=True)
        attn = jnp.where(full_mask[:, None, None, :], attn, -jnp.finfo(attn.dtype).max)
        attn = jax.nn.softmax(attn, axis=-1)
        out = jnp.einsum('bhij,bhjd->bhid', attn, v)
        out = out.transpose(0, 2, 1, 3).reshape(b, m, INNER)
        return out @ Wo.T + bo

    def _L1_ffn_ref(x, W1, b1, W2, b2, Wr, br):
        import jax, jax.numpy as jnp
        import numpy as np
        from jax import lax
        D = 256
        H = 1024
        E = 8
        TOPK = 2
        B, S, _ = x.shape
        xf = x.reshape(-1, D)
        logits = xf @ Wr + br
        topv, _ = lax.top_k(logits, TOPK)
        thresh = topv[:, TOPK - 1:TOPK]
        masked = jnp.where(logits >= thresh, logits, -jnp.inf)
        weights = jax.nn.softmax(masked, axis=-1)
        h = jax.nn.gelu(jnp.einsum('td,edh->eth', xf, W1) + b1[:, None, :], approximate=False)
        expert_out = jnp.einsum('eth,ehd->etd', h, W2) + b2[:, None, :]
        out = jnp.einsum('etd,te->td', expert_out, weights)
        return out.reshape(B, S, D)
    x = x + _L0_xattn_ref(_layernorm(x, axis=-1), ctx_768, L0_xattn_W_Q, L0_xattn_W_K, L0_xattn_W_V, L0_xattn_W_O, L0_xattn_ln_lat_g, L0_xattn_ln_lat_b, L0_xattn_ln_in_g, L0_xattn_ln_in_b)
    x = x + _L0_ffn_ref(_layernorm(x, axis=-1), L0_ffn_Wg, L0_ffn_routing_bias, L0_ffn_W1, L0_ffn_W2, L0_ffn_W3, L0_ffn_Ws1, L0_ffn_Ws2, L0_ffn_Ws3)
    x = x + _L1_xattn_ref(ctx_768, _layernorm(x, axis=-1), mask_BxS2_bk0, L1_xattn_ln_x_g, L1_xattn_ln_x_b, L1_xattn_ln_l_g, L1_xattn_ln_l_b, L1_xattn_qn_g, L1_xattn_kn_g, L1_xattn_Wq, L1_xattn_Wkv, L1_xattn_Wlkv, L1_xattn_Wo, L1_xattn_bo)
    x = x + _L1_ffn_ref(_layernorm(x, axis=-1), L1_ffn_W1, L1_ffn_b1, L1_ffn_W2, L1_ffn_b2, L1_ffn_Wr, L1_ffn_br)
    return x

_drawn_inputs = setup_inputs


def setup_inputs(seed=0):
    import zlib

    import numpy as np

    out = dict(_drawn_inputs(seed))
    spreads = {'L0_xattn_ln_lat_g': (1.0, 0.2),
     'L0_xattn_ln_lat_b': (0.0, 0.1),
     'L0_xattn_ln_in_g': (1.0, 0.2),
     'L0_xattn_ln_in_b': (0.0, 0.1),
     'L0_ffn_routing_bias': (0.0, 0.8),
     'L1_xattn_ln_x_g': (1.0, 0.6),
     'L1_xattn_ln_x_b': (0.0, 0.8),
     'L1_xattn_ln_l_g': (1.0, 0.2),
     'L1_xattn_ln_l_b': (0.0, 0.1),
     'L1_xattn_qn_g': (1.0, 0.6),
     'L1_xattn_kn_g': (1.0, 0.6),
     'L1_xattn_bo': (0.0, 0.1),
     'L1_ffn_b1': (0.0, 0.403),
     'L1_ffn_b2': (0.0, 0.335),
     'L1_ffn_br': (0.0, 0.319)}
    factors = {'L0_ffn_Wg': 5.545,
     'L0_ffn_W1': 4.266,
     'L0_ffn_W2': 4.262,
     'L0_ffn_W3': 4.266,
     'L1_xattn_Wkv': 2.827,
     'L0_ffn_Ws1': 3.875,
     'L0_ffn_Ws2': 3.699,
     'L0_ffn_Ws3': 3.768}
    for name, (base, spread) in spreads.items():
        noise = np.random.default_rng([zlib.crc32(name.encode()), seed]).standard_normal(out[name].shape)
        drawn = base * np.exp(spread * noise) if base else spread * noise
        out[name] = jnp.asarray(drawn.astype(out[name].dtype))
    for name, factor in factors.items():
        out[name] = (out[name] * factor).astype(out[name].dtype)
    return out
```

```python
import concourse.bass as bass
from concourse import mybir
from contextlib import ExitStack

FP32 = mybir.dt.float32
FP32R = mybir.dt.float32r
UINT8 = mybir.dt.uint8
ALU = mybir.AluOpType
ACT = mybir.ActivationFunctionType
AX = mybir.AxisListType

P = 128
B, S, D = 2, 1024, 256
T = B * S
NT = T // P
KD = D // P
BLK = 512
NB = T // BLK
TPB = BLK // P
SC, DC = 77, 192
HC = DC // 2
EPS = 1e-5
H0 = 8
DH0 = D // H0
G0 = P // DH0
KC0 = H0 * SC
NC0 = -(-KC0 // P)
E = 8
H_FF0 = D * 2 * 4 // 3
CH0 = H_FF0 // P
REM0 = H_FF0 - CH0 * P
MIX0 = P // REM0
NMIX0 = (E + 1) // MIX0
TOPK0 = 4
H1 = 4
DH1 = D // H1
SCP = SC + 1
NKT = S // P + 1
NK1 = S + SCP
NEG = -(2.0 - 2.0 ** -11) * 2.0 ** 127
H_FF1 = 1024
CH1 = H_FF1 // P
TOPK1 = 2


def split_passes(hi_lo_stationary, hi_lo_moving):
    (sh, sl), (mh, ml) = hi_lo_stationary, hi_lo_moving
    return ((sh, mh), (sh, ml), (sl, mh))


class Chain:

    def __init__(self, eng, sem, n=0):
        self.eng, self.sem, self.n = eng, sem, n

    def mark(self, instruction):
        instruction.then_inc(self.sem, 1)
        self.n += 1

    def wait(self):
        self.eng.wait_ge(self.sem, self.n)


class Memory:

    def __init__(self, nc, ctx):
        def sb(name, shape, dt=FP32):
            return ctx.enter_context(nc.sbuf_tensor(name, shape, dt))

        self.ps = ctx.enter_context(nc.psum_tensor("ps", [P, 8, BLK], FP32))
        self.x = sb("x_resid", [P, NT, D])
        self.ident = sb("ident", [P, P])
        self.uh = sb("uh", [P, KD, T], FP32R)
        self.ul = sb("ul", [P, KD, T], FP32R)
        self.z = sb("z", [P, 2, TPB, D])
        self.st = sb("st", [P, NT, 6])
        self.mv = sb("mv", [P, NT, 2])
        self.rs = sb("rs", [P, 4, NT])
        self.mhalf = sb("mhalf", [P, NT])
        self.one = sb("one", [P, 1])
        self.cxh = sb("cxh", [HC, 2, B, SCP], FP32R)
        self.cxl = sb("cxl", [HC, 2, B, SCP], FP32R)
        self.norm = NormSems(nc, ctx)
        self.raw = sb("raw", [P, CH1 * 4 * P + CH1])


class NormSems:

    def __init__(self, nc, ctx):
        def sem(name):
            return ctx.enter_context(nc.semaphore(f"norm_{name}"))

        self.blocks = self.affine_blocks = self.pool_marks = 0

        self.var = sem("var")
        self.rs = sem("rs")
        self.z = sem("z")
        self.zt = sem("zt")
        self.zf = sem("zf")
        self.hi = sem("hi")
        self.lo = sem("lo")
        self.dch = sem("dch")
        self.pch = sem("pch")

    def next(self, twice, affine):
        self.blocks += NB
        self.affine_blocks += NB * affine
        self.pool_marks += NB * (6 if twice else 1)



def norm_dve(dve, m, s, affine=None, zf=None):
    n0, a0 = s.blocks, s.affine_blocks
    ch = Chain(dve, s.dch, n0 * TPB)
    for blk in range(NB):
        for j in range(TPB):
            t = blk * TPB + j
            ch.mark(dve.bn_stats(m.st[:, t, :], m.x[:, t, :]))
        ch.wait()
        for j in range(TPB):
            t = blk * TPB + j
            i = dve.bn_aggr(m.mv[:, t, :], m.st[:, t, :])
        i.then_inc(s.var, 1)

    def normalise(blk):
        dve.wait_ge(s.rs, n0 + blk + 1)
        if blk >= 2:
            dve.wait_ge(s.zt, n0 + blk - 1)
        for j in range(TPB):
            t = blk * TPB + j
            i = dve.tensor_scalar(m.z[:, blk % 2, j, :], m.x[:, t, :], m.mv[:, t, 0:1],
                                  m.rs[:, 3, t:t + 1], ALU.subtract, ALU.mult)
        i.then_inc(s.z, 1)

    def lower_half(blk):
        bank = 2 * (blk % 2)
        cols = slice(blk * BLK, (blk + 1) * BLK)
        src = m.ps[:, bank:bank + KD, :]
        if affine is not None:
            dve.wait_ge(s.zt, n0 + blk + 1)
            if blk:
                dve.wait_ge(s.lo, n0 + blk)
            for k in range(KD):
                i = dve.tensor_scalar(zf[:, k, :], m.ps[:, bank + k, :], affine[:, 0, k:k + 1],
                                      affine[:, 1, k:k + 1], ALU.mult, ALU.add)
            i.then_inc(s.zf, 1)
            src = zf[:, :, :]
        dve.wait_ge(s.hi, n0 + blk + 1)
        dve.tensor_tensor(m.ul[:, :, cols], src, m.uh[:, :, cols].bitcast(FP32),
                          ALU.subtract).then_inc(s.lo, 1)

    normalise(0)
    for blk in range(NB):
        if blk + 1 < NB:
            normalise(blk + 1)
        lower_half(blk)


def norm_pool(pool, m, s, twice):
    n0 = s.blocks
    ch = Chain(pool, s.pch, s.pool_marks)
    for blk in range(NB):
        c = slice(blk * TPB, (blk + 1) * TPB)
        var, half = m.mv[:, c, 1], m.mhalf[:, c]
        tmp, r1, tmp2, r = (m.rs[:, n, c] for n in range(4))
        pool.wait_ge(s.var, n0 + blk + 1)
        ch.mark(pool.tensor_scalar(tmp, var, EPS, None, ALU.add))
        ch.wait()
        if not twice:
            pool.tensor_tensor(r, tmp, half, ALU.pow).then_inc(s.rs, 1)
            continue
        ch.mark(pool.tensor_tensor(r1, tmp, half, ALU.pow))
        ch.wait()
        ch.mark(pool.tensor_tensor(tmp, r1, r1, ALU.mult))
        ch.wait()
        ch.mark(pool.tensor_tensor(tmp2, tmp, var, ALU.mult))
        ch.wait()
        ch.mark(pool.tensor_scalar(tmp, tmp2, EPS, None, ALU.add))
        ch.wait()
        ch.mark(pool.tensor_tensor(tmp2, tmp, half, ALU.pow))
        ch.wait()
        pool.tensor_tensor(r, tmp2, r1, ALU.mult).then_inc(s.rs, 1)


def norm_pe(pe, m, s):
    n0 = s.blocks
    for blk in range(NB):
        bank = 2 * (blk % 2)
        pe.wait_ge(s.z, n0 + blk + 1)
        if blk >= 2:
            pe.wait_ge(s.lo, n0 + blk - 1)
        for k in range(KD):
            for j in range(TPB):
                i = pe.transpose(m.ps[:, bank + k, j * P:(j + 1) * P],
                                 m.z[:, blk % 2, j, k * P:(k + 1) * P], m.ident[:, :])
        i.then_inc(s.zt, 1)


def norm_act(act, m, s, zf=None):
    n0, a0 = s.blocks, s.affine_blocks
    for blk in range(NB):
        bank = 2 * (blk % 2)
        cols = slice(blk * BLK, (blk + 1) * BLK)
        if zf is None:
            act.wait_ge(s.zt, n0 + blk + 1)
            act.activation(m.uh[:, :, cols], m.ps[:, bank:bank + KD, :], ACT.Copy).then_inc(s.hi, 1)
        else:
            act.wait_ge(s.zf, a0 + blk + 1)
            act.activation(m.uh[:, :, cols], zf[:, :, :], ACT.Copy).then_inc(s.hi, 1)



def attention0(nc, m, a, raw_in):
    ps = m.ps
    with ExitStack() as ctx:
        def sb(name, shape, dt=FP32):
            return ctx.enter_context(nc.sbuf_tensor(name, shape, dt))

        def sem(name):
            return ctx.enter_context(nc.semaphore(name))

        wqh, wql = (sb(f"wq0{n}", [P, KD, D], FP32R) for n in "hl")
        woh, wol = (sb(f"wo0{n}", [P, KD, D], FP32R) for n in "hl")
        kbh, kbl = (sb(f"kb0{n}", [P, B, KD, G0, SC], FP32R) for n in "hl")
        vbh, vbl = (sb(f"vb0{n}", [P, B, NC0, D], FP32R) for n in "hl")
        lat_gb = sb("lat_gb", [P, 2, KD])

        with ExitStack() as c2:
            def sb2(name, shape, dt=FP32):
                return c2.enter_context(nc.sbuf_tensor(name, shape, dt))

            wraw = m.raw[:, 0:4 * D].rearrange("p (w k n) -> p w k n", w=2, k=KD)
            craw = sb2("craw", [HC, 2, 2, D])
            wkh, wkl = (sb2(f"wkv0{n}", [HC, 2, 2, D], FP32R) for n in "hl")
            cx = sb2("cx", [SC, B, DC])
            cn = sb2("cn", [SC, B, DC])
            cst = sb2("cst", [SC, B, 6])
            cmv = sb2("cmv", [SC, B, 2])
            crs = sb2("crs", [SC, 2, B])
            in_gb = sb2("in_gb", [HC, 2, 2])
            lx_gb = sb2("lx_gb", [HC, 2, 2])
            cf = sb2("cf", [HC, 2, 2, B, SC])
            c0h, c0l = (sb2(f"c0{n}", [HC, 2, B, SC], FP32R) for n in "hl")
            reph, repl = (sb2(f"rep{n}", [HC, 2, B, NC0 * P], FP32R) for n in "hl")
            bd = sb2("bd", [P, NC0, D])
            vf = sb2("vf", [P, B, NC0, D])

            s_cx, s_par, s_w, s_xl = sem("a0_cx"), sem("a0_par"), sem("a0_w"), sem("a0_xl")
            s_var, s_rs, s_cn, s_ct = sem("a0_var"), sem("a0_rs"), sem("a0_cn"), sem("a0_ct")
            s_cf, s_ch, s_cl, s_rep = sem("a0_cf"), sem("a0_ch"), sem("a0_cl"), sem("a0_rep")
            s_zero, s_wh, s_wl = sem("a0_zero"), sem("a0_wh"), sem("a0_wl")
            s_kt, s_kh, s_kl = sem("a0_kt"), sem("a0_kh"), sem("a0_kl")
            s_v, s_vf, s_vh, s_vl = sem("a0_v"), sem("a0_vf"), sem("a0_vh"), sem("a0_vl")
            s_pch = sem("a0_pch")

            with nc.Block() as block:
                @block.sync
                def _(sp):
                    sp.dma_start(cx[:], a["ctx_768"].rearrange("b s d -> s b d")).then_inc(s_cx, 16)
                    sp.dma_start(m.ident[:], a["c_ident"]).then_inc(s_cx, 16)
                    sp.dma_start(in_gb[:], a["in_gb"]).then_inc(s_par, 16)
                    sp.dma_start(lx_gb[:], a["lx_gb"]).then_inc(s_par, 16)
                    sp.dma_start(craw[:], a["wkv0"]).then_inc(s_w, 16)
                    sp.dma_start(bd[:], a["c_bd"]).then_inc(s_par, 16)
                    sp.dma_start(lat_gb[:], a["lat_gb"]).then_inc(s_par, 16)
                    xv = a["x"].rearrange("b (t p) d -> p (b t) d", p=P)
                    for blk in range(NB):
                        c = slice(blk * TPB, (blk + 1) * TPB)
                        sp.dma_start(m.x[:, c, :], xv[:, c, :]).then_inc(s_xl, 16)
                    sp.wait_ge(s_xl, 16 * NB)

                @block.gpsimd
                def _(pool):
                    ch = Chain(pool, s_pch)
                    pool.memset(m.mhalf[:], -0.5).then_inc(s_zero, 1)
                    pool.memset(m.one[:], 1.0)
                    for t in (m.cxh, m.cxl, reph, repl, kbh, kbl):
                        pool.memset(t[:].bitcast(FP32), 0.0).then_inc(s_zero, 1)
                    pool.wait_ge(s_var, 1)
                    pool.wait_ge(s_zero, 1)
                    ch.mark(pool.tensor_scalar(crs[:, 0, :], cmv[:, :, 1], EPS, None, ALU.add))
                    ch.wait()
                    pool.tensor_tensor(crs[:, 1, :], crs[:, 0, :], m.mhalf[0:SC, 0:B], ALU.pow)\
                        .then_inc(s_rs, 1)
                    pool.wait_ge(s_w, 32)
                    pool.wait_ge(s_wh, 1)
                    pool.tensor_tensor(wkl[:], craw[:], wkh[:].bitcast(FP32), ALU.subtract).then_inc(s_wl, 1)
                    pool.wait_ge(s_wh, 3)
                    pool.tensor_tensor(wql[:], wraw[:, 0], wqh[:].bitcast(FP32), ALU.subtract).then_inc(s_wl, 1)
                    pool.tensor_tensor(wol[:], wraw[:, 1], woh[:].bitcast(FP32), ALU.subtract).then_inc(s_wl, 1)

                @block.scalar
                def _(act):
                    act.dma_start(wraw, a["wqo0"]).then_inc(s_w, 16)
                    act.wait_ge(s_w, 32)
                    act.activation(wkh[:], craw[:], ACT.Copy).then_inc(s_wh, 1)
                    act.wait_ge(s_cf, 1)
                    act.activation(c0h[:], cf[:, 0], ACT.Copy).then_inc(s_ch, 1)
                    act.wait_ge(s_cf, 2)
                    act.wait_ge(s_zero, 3)
                    act.activation(m.cxh[:, :, :, 0:SC], cf[:, 1], ACT.Copy).then_inc(s_ch, 1)
                    act.activation(wqh[:], wraw[:, 0], ACT.Copy).then_inc(s_wh, 1)
                    act.activation(woh[:], wraw[:, 1], ACT.Copy).then_inc(s_wh, 1)
                    act.wait_ge(s_kt, 1)
                    act.wait_ge(s_zero, 7)
                    for g in range(KD):
                        for j in range(G0):
                            r = slice(j * DH0, (j + 1) * DH0)
                            act.activation(kbh[r, :, g, j, :],
                                           ps[r, 1, g * B * SC:(g + 1) * B * SC]
                                           .rearrange("p (b k) -> p b k", b=B), ACT.Copy).then_inc(s_kh, 1)
                    for b in range(B):
                        act.wait_ge(s_vf, b + 1)
                        act.activation(vbh[:, b], vf[:, b], ACT.Copy).then_inc(s_vh, 1)

                @block.vector
                def _(dve):
                    dve.wait_ge(s_cx, 32)
                    for b in range(B):
                        dve.bn_stats(cst[:, b, :], cx[:, b, :]).then_inc(s_cn, 1)
                    dve.wait_ge(s_cn, 2)
                    for b in range(B):
                        i = dve.bn_aggr(cmv[:, b, :], cst[:, b, :])
                    i.then_inc(s_var, 1)
                    dve.wait_ge(s_rs, 1)
                    for b in range(B):
                        dve.tensor_scalar(cn[:, b, :], cx[:, b, :], cmv[:, b, 0:1], crs[:, 1, b:b + 1],
                                          ALU.subtract, ALU.mult).then_inc(s_cn, 1)
                    dve.wait_ge(s_ct, 1)
                    dve.wait_ge(s_par, 64)
                    for w, gb in enumerate((in_gb, lx_gb)):
                        for k in range(2):
                            i = dve.tensor_scalar(cf[:, w, k].rearrange("p b s -> p (b s)"),
                                                  ps[0:HC, 0, k * B * SC:(k + 1) * B * SC],
                                                  gb[:, 0, k:k + 1], gb[:, 1, k:k + 1], ALU.mult, ALU.add)
                        i.then_inc(s_cf, 1)
                    dve.wait_ge(s_ch, 1)
                    dve.tensor_tensor(c0l[:], cf[:, 0], c0h[:].bitcast(FP32), ALU.subtract).then_inc(s_cl, 1)
                    dve.wait_ge(s_ch, 2)
                    dve.wait_ge(s_zero, 5)
                    dve.tensor_tensor(m.cxl[:, :, :, 0:SC], cf[:, 1], m.cxh[:, :, :, 0:SC].bitcast(FP32),
                                      ALU.subtract).then_inc(s_cl, 1)
                    dve.wait_ge(s_cl, 1)
                    for src, dst in ((c0h, reph), (c0l, repl)):
                        for k in range(2):
                            for b in range(B):
                                dve.tensor_copy(dst[:, k, b, 0:KC0].rearrange("p (h s) -> p h s", h=H0),
                                                src[:, k, b:b + 1, :].to_broadcast([HC, H0, SC])
                                                .bitcast(FP32)).then_inc(s_rep, 1)
                    dve.wait_ge(s_kh, KD * G0)
                    for g in range(KD):
                        for j in range(G0):
                            r = slice(j * DH0, (j + 1) * DH0)
                            dve.tensor_tensor(kbl[r, :, g, j, :],
                                              ps[r, 1, g * B * SC:(g + 1) * B * SC]
                                              .rearrange("p (b k) -> p b k", b=B),
                                              kbh[r, :, g, j, :].bitcast(FP32), ALU.subtract).then_inc(s_kl, 1)
                    psv = ps[:, 2:7, :].rearrange("p k n -> p (k n)")
                    dve.wait_ge(s_v, B)
                    for b in range(B):
                        dve.tensor_tensor(vf[:, b].rearrange("p c n -> p (c n)"),
                                          psv[:, b * NC0 * D:(b + 1) * NC0 * D],
                                          bd[:].rearrange("p c n -> p (c n)"), ALU.mult).then_inc(s_vf, 1)
                    for b in range(B):
                        dve.wait_ge(s_vf, b + 1)
                        dve.wait_ge(s_vh, b + 1)
                        dve.tensor_tensor(vbl[:, b], vf[:, b], vbh[:, b].bitcast(FP32),
                                          ALU.subtract).then_inc(s_vl, 1)

                @block.tensor
                def _(pe):
                    pe.wait_ge(s_cx, 32)
                    pe.wait_ge(s_cn, 4)
                    for k in range(2):
                        for b in range(B):
                            o = (k * B + b) * SC
                            i = pe.transpose(ps[0:HC, 0, o:o + SC], cn[:, b, k * HC:(k + 1) * HC],
                                             m.ident[0:SC, 0:SC])
                    i.then_inc(s_ct, 1)
                    pe.wait_ge(s_wl, 1)
                    pe.wait_ge(s_cl, 1)
                    for g in range(KD):
                        n = 0
                        for k in range(2):
                            for st, mo in split_passes((wkh, wkl), (c0h, c0l)):
                                i = pe.matmul(ps[:, 1, g * B * SC:(g + 1) * B * SC],
                                              st[:, 0, k, g * P:(g + 1) * P],
                                              mo[:, k].rearrange("p b s -> p (b s)"),
                                              start=n == 0, stop=n == 5)
                                n += 1
                    i.then_inc(s_kt, 1)
                    pe.wait_ge(s_rep, 8)
                    for b in range(B):
                        for c in range(NC0):
                            u = b * NC0 + c
                            n = 0
                            for k in range(2):
                                for st, mo in split_passes((reph, repl), (wkh, wkl)):
                                    i = pe.matmul(ps[:, 2 + u // 2, (u % 2) * D:(u % 2 + 1) * D],
                                                  st[:, k, b, c * P:(c + 1) * P], mo[:, 1, k, :],
                                                  start=n == 0, stop=n == 5)
                                    n += 1
                        i.then_inc(s_v, 1)

        qh, ql = (sb(f"q0{n}", [P, KD, T], FP32R) for n in "hl")
        zf = sb("zf", [P, KD, BLK])
        mx = sb("mx", [P, 2, H0])
        sm = sb("sm", [P, 2, H0])
        rc = sb("rc", [P, 2, H0])
        sd = sb("sd", [P, 2, H0, SC])
        ex = sb("ex", [P, 2, H0, SC])
        pn = sb("pn", [P, 2, KC0])
        pth, ptl = (sb(f"pt{n}", [P, NC0, BLK], FP32R) for n in "hl")
        oh, ol = (sb(f"o0{n}", [P, KD, BLK], FP32R) for n in "hl")
        ns = m.norm
        s_q, s_qh, s_ql = sem("a_q"), sem("a_qh"), sem("a_ql")
        s_s, s_mx, s_sd, s_e, s_sum, s_rc, s_pn = (sem(f"a_{n}") for n in ("s", "mx", "sd", "e", "sum", "rc", "pn"))
        s_pt, s_pth, s_ptl = sem("a_pt"), sem("a_pth"), sem("a_ptl")
        s_o, s_oh, s_ol, s_y, s_x = (sem(f"a_{n}") for n in ("o", "oh", "ol", "y", "x"))
        scale = float(DH0) ** -0.5
        last_rows = KC0 - (NC0 - 1) * P
        halves = [(0, 3), (2, 5)]

        def tiles():
            return [(t // TPB, t % TPB, t) for t in range(NT)]

        with nc.Block() as block:
            @block.sync
            def _(sp):
                sp.dma_start(m.raw[:, 0:CH0 * 6 * P], a["f0_w"][0]).then_inc(raw_in, 16)

            @block.gpsimd
            def _(pool):
                norm_pool(pool, m, ns, twice=True)
                for blk, j, t in tiles():
                    pool.wait_ge(s_rc, t + 1)
                    if t >= 2:
                        pool.wait_ge(s_pt, t - 1)
                    pool.tensor_tensor(pn[:, t % 2].rearrange("p (h s) -> p h s", h=H0), ex[:, t % 2],
                                       rc[:, t % 2].unsqueeze(2).to_broadcast([P, H0, SC]),
                                       ALU.mult).then_inc(s_pn, 1)

            @block.scalar
            def _(act):
                norm_act(act, m, ns, zf)
                for n in range(NB * KD):
                    blk, g = n // KD, n % KD
                    act.wait_ge(s_q, n + 1)
                    act.activation(qh[:, g, blk * BLK:(blk + 1) * BLK], ps[:, 4 + n % 4, :], ACT.Copy)\
                        .then_inc(s_qh, 1)

                def exps(t):
                    act.wait_ge(s_sd, t + 1)
                    if t >= 2:
                        act.wait_ge(s_pn, t - 1)
                    act.activation(ex[:, t % 2], sd[:, t % 2], ACT.Exp, scale=scale).then_inc(s_e, 1)

                exps(0)
                for blk, j, t in tiles():
                    if t + 1 < NT:
                        exps(t + 1)
                    act.wait_ge(s_pt, t + 1)
                    if j == 0 and blk:
                        act.wait_ge(s_o, blk)
                    c = slice(j * P, (j + 1) * P)
                    act.activation(pth[:, 0:4, c], ps[:, 4, :].rearrange("p (c n) -> p c n", c=4), ACT.Copy)
                    act.activation(pth[0:last_rows, 4, c], ps[0:last_rows, 5, 0:P], ACT.Copy).then_inc(s_pth, 1)
                    if j == TPB - 1:
                        act.wait_ge(s_o, blk + 1)
                        if blk:
                            act.wait_ge(s_y, 2 * blk)
                        act.activation(oh[:], ps[:, 6:8, :], ACT.Copy).then_inc(s_oh, 1)

            @block.vector
            def _(dve):
                norm_dve(dve, m, ns, lat_gb, zf)
                for n in range(NB * KD):
                    blk, g = n // KD, n % KD
                    c = slice(blk * BLK, (blk + 1) * BLK)
                    dve.wait_ge(s_qh, n + 1)
                    dve.tensor_tensor(ql[:, g, c], ps[:, 4 + n % 4, :], qh[:, g, c].bitcast(FP32),
                                      ALU.subtract).then_inc(s_ql, 1)

                def shift(t):
                    sl = 2 * (t % 2)
                    sv = ps[:, sl:sl + 2, 0:G0 * SC].rearrange("p g (h s) -> p g h s", h=G0)
                    dve.wait_ge(s_s, t + 1)
                    dve.reduce_max(mx[:, t % 2].rearrange("p (g h) -> p g h", g=KD), sv, AX.X)\
                        .then_inc(s_mx, 1)
                    dve.wait_ge(s_mx, t + 1)
                    if t >= 2:
                        dve.wait_ge(s_e, t - 1)
                    for g in range(KD):
                        i = dve.tensor_tensor(sd[:, t % 2, g * G0:(g + 1) * G0, :], sv[:, g],
                                              mx[:, t % 2, g * G0:(g + 1) * G0].unsqueeze(2)
                                              .to_broadcast([P, G0, SC]), ALU.subtract)
                    i.then_inc(s_sd, 1)

                def sums(t):
                    dve.wait_ge(s_e, t + 1)
                    dve.reduce_sum(sm[:, t % 2], ex[:, t % 2], AX.X).then_inc(s_sum, 1)
                    dve.wait_ge(s_sum, t + 1)
                    if t >= 2:
                        dve.wait_ge(s_pn, t - 1)
                    dve.reciprocal(rc[:, t % 2], sm[:, t % 2]).then_inc(s_rc, 1)

                shift(0)
                for blk, j, t in tiles():
                    if t + 1 < NT:
                        shift(t + 1)
                    if t == 0:
                        sums(0)
                    if t + 1 < NT:
                        sums(t + 1)
                    dve.wait_ge(s_pth, t + 1)
                    c = slice(j * P, (j + 1) * P)
                    dve.tensor_tensor(ptl[:, 0:4, c], ps[:, 4, :].rearrange("p (c n) -> p c n", c=4),
                                      pth[:, 0:4, c].bitcast(FP32), ALU.subtract)
                    dve.tensor_tensor(ptl[0:last_rows, 4, c], ps[0:last_rows, 5, 0:P],
                                      pth[0:last_rows, 4, c].bitcast(FP32), ALU.subtract).then_inc(s_ptl, 1)
                    if j == TPB - 1:
                        dve.wait_ge(s_oh, blk + 1)
                        dve.tensor_tensor(ol[:], ps[:, 6:8, :], oh[:].bitcast(FP32), ALU.subtract)\
                            .then_inc(s_ol, 1)
                        for h in range(2):
                            tt = blk * TPB + 2 * h
                            dve.wait_ge(s_y, 2 * blk + h + 1)
                            xs = m.x[:, tt:tt + 2, :]
                            dve.tensor_tensor(xs, xs, ps[:, 6 + h, :].rearrange("p (t n) -> p t n", t=2),
                                              ALU.add).then_inc(s_x, 1)

            @block.tensor
            def _(pe):
                norm_pe(pe, m, ns)
                for n in range(NB * KD):
                    blk, g = n // KD, n % KD
                    pe.wait_ge(ns.lo, ns.blocks + blk + 1)
                    if n >= 4:
                        pe.wait_ge(s_ql, n - 3)
                    k3 = 0
                    for k in range(KD):
                        for st, mo in split_passes((wqh, wql), (m.uh, m.ul)):
                            i = pe.matmul(ps[:, 4 + n % 4, :], st[:, k, g * P:(g + 1) * P],
                                          mo[:, k, blk * BLK:(blk + 1) * BLK], start=k3 == 0, stop=k3 == 5)
                            k3 += 1
                    i.then_inc(s_q, 1)

                def scores(t):
                    b = t // (NT // B)
                    if t == 0:
                        pe.wait_ge(s_ql, NB * KD)
                    if t >= 2:
                        pe.wait_ge(s_sd, t - 1)
                    for g in range(KD):
                        for n, (st, mo) in enumerate(split_passes((qh, ql), (kbh, kbl))):
                            i = pe.matmul(ps[:, 2 * (t % 2) + g, 0:G0 * SC], st[:, g, t * P:(t + 1) * P],
                                          mo[:, b, g].rearrange("p h s -> p (h s)"), start=n == 0, stop=n == 2)
                    i.then_inc(s_s, 1)

                scores(0)
                for blk, j, t in tiles():
                    b = t // (NT // B)
                    if t + 1 < NT:
                        scores(t + 1)
                    pe.wait_ge(s_pn, t + 1)
                    if t:
                        pe.wait_ge(s_ptl, t)
                    for c in range(NC0):
                        n = min(P, KC0 - c * P)
                        i = pe.transpose(ps[0:n, 4 + c // 4, (c % 4) * P:(c % 4 + 1) * P],
                                         pn[:, t % 2, c * P:c * P + n], m.ident[:, :])
                    i.then_inc(s_pt, 1)
                    if j == TPB - 1:
                        pe.wait_ge(s_ptl, t + 1)
                        if blk:
                            pe.wait_ge(s_x, 2 * blk)
                        for g, (c0, c1) in enumerate(halves):
                            for c in range(c0, c1):
                                r = min(P, KC0 - c * P)
                                for n, (st, mo) in enumerate(split_passes((vbh, vbl), (pth, ptl))):
                                    i = pe.matmul(ps[:, 6 + g, :], st[0:r, b, c, g * P:(g + 1) * P],
                                                  mo[0:r, c, :], start=c == c0 and n == 0,
                                                  stop=c == c1 - 1 and n == 2)
                        i.then_inc(s_o, 1)
                        pe.wait_ge(s_ol, blk + 1)
                        for jj in range(TPB):
                            n = 0
                            for g in range(KD):
                                for st, mo in split_passes((oh, ol), (woh, wol)):
                                    i = pe.matmul(ps[:, 6 + jj // 2, (jj % 2) * D:(jj % 2 + 1) * D],
                                                  st[:, g, jj * P:(jj + 1) * P], mo[:, g, :],
                                                  start=n == 0, stop=n == 5)
                                    n += 1
                            if jj % 2:
                                i.then_inc(s_y, 1)



class Step:

    def __init__(self, n, group, chunk, blk, block, ends, mixed=False):
        self.n = n
        self.group = group
        self.chunk, self.blk = chunk, blk
        self.block = block
        self.first, self.last = chunk == 0, ends
        self.mixed = mixed


class Base:

    def __init__(self, lay, i):
        self.at_start = isinstance(i, int) and i == 0
        self.pair = i
        self.n = i * len(lay.body)
        self.block = i * 2 * NB
        self.group = i * 2
        self.chunk = i * 2 * lay.chunks


class Layer:
    def __init__(self, gated, chunks, pairs, tail_chunks):
        self.gated = gated
        self.chunks = chunks
        self.width = (4 + 2 if gated else 2 + 2) * P
        self.body = self.steps([chunks, chunks])
        self.tail = self.steps(tail_chunks, mixed=tail_chunks[1] != chunks)
        self.pairs = pairs
        self.hbanks = 2 if gated else 4

    def steps(self, chunks, mixed=False):
        out = []
        for g, nc_ in enumerate(chunks):
            for blk in range(NB):
                for c in range(nc_):
                    out.append(Step(len(out), g, c, blk, g * NB + blk, c == nc_ - 1, mixed and g == 1))
        return out


def walk(lay, eng, lead, early, late):

    def some(steps, base, after, base_after):
        for st in steps:
            ahead = st.n + lead
            if ahead < len(steps):
                early(steps[ahead], base)
            elif after:
                early(after[ahead - len(steps)], base_after)
            late(st, base)

    for st in lay.body[:lead]:
        early(st, Base(lay, 0))
    some(lay.body, Base(lay, 0), lay.body, Base(lay, 1))
    with eng.Fori(1, lay.pairs) as i:
        some(lay.body, Base(lay, i), lay.body, Base(lay, i + 1))
    some(lay.tail, Base(lay, lay.pairs), None, None)


def experts(nc, m, a, tag, lay, raw_in):
    ps = m.ps
    gated, CH, W = lay.gated, lay.chunks, lay.width
    n_in = 2 if gated else 1
    lead_w = P * KD * n_in
    w_dram = a[f"{tag}_w"]
    with ExitStack() as ctx:
        def sb(name, shape, dt=FP32):
            return ctx.enter_context(nc.sbuf_tensor(f"{tag}_{name}", shape, dt))

        def sem(name):
            return ctx.enter_context(nc.semaphore(f"{tag}_{name}"))

        wh, wl = (sb(f"w{n}", [P, 2, CH * W], FP32R) for n in "hl")
        yT = sb("yT", [P, KD, T])
        bcol = sb("bcol", [P, 2, CH]) if not gated else None
        g_dram = nc.dram_tensor(f"{tag}_gate_rows", [E + 1, T], FP32).ap()
        s_split, s_wh = sem("split"), sem("wh")
        s_gd = sem("gd")

        def split(pool, group, chunk, par):
            c = slice(chunk * W, (chunk + 1) * W)
            pool.tensor_tensor(wh[:, par, c], m.raw[:, c], m.one[:].to_broadcast([P, W]), ALU.mult).then_inc(s_wh, 1)
            pool.wait_ge(s_wh, group * CH + chunk + 1)
            pool.tensor_tensor(wl[:, par, c], m.raw[:, c], wh[:, par, c].bitcast(FP32), ALU.subtract)\
                .then_inc(s_split, 1)

        with ExitStack() as c2:
            def sb2(name, shape, dt=FP32):
                return c2.enter_context(nc.sbuf_tensor(f"{tag}_{name}", shape, dt))

            wg = sb2("wg", [P, KD, E])
            wgh, wgl = (sb2(f"wg{n}", [P, KD, E], FP32R) for n in "hl")
            bias = sb2("bias", [P, E])
            tri = sb2("tri", [P, E, E]) if gated else None
            b2 = sb2("b2", [E, D]) if not gated else None
            lg = sb2("lg", [P, NT, E])
            gt = sb2("gt", [P, NT, E, E])
            eq = sb2("eq", [P, NT, E, E]) if gated else None
            rank = sb2("rank", [P, NT, E])
            mk = sb2("mk", [P, NT, E])
            mx = sb2("mx", [P, NT])
            sh = sb2("sh", [P, NT, E])
            ex = sb2("ex", [P, NT, E])
            em = sb2("em", [P, NT, E])
            sm = sb2("sm", [P, NT])
            rc = sb2("rc", [P, NT])
            w = sb2("w", [P, NT, E + 1])
            wT = sb2("wT", [E + 1, T])
            ns = m.norm
            s_par, s_wg, s_lg, s_sh, s_ex, s_w, s_wt, s_wTs, s_b2, s_y0 = (
                sem(f"r_{n}") for n in ("par", "wg", "lg", "sh", "ex", "w", "wt", "wTs", "b2", "y0"))
            s_ch = sem("r_ch")
            n_par = 3 if gated else 3

            with nc.Block() as block:
                @block.sync
                def _(sp):
                    sp.dma_start(wg[:], a[f"{tag}_wg"]).then_inc(s_par, 16)
                    sp.dma_start(bias[:], a[f"{tag}_bias"].partition_broadcast(P)).then_inc(s_par, 16)
                    if gated:
                        sp.dma_start(tri[:], a["c_tri"].partition_broadcast(P)).then_inc(s_par, 16)
                    else:
                        sp.dma_start(b2[:], a[f"{tag}_b2"]).then_inc(s_par, 16)
                    sp.wait_ge(s_wTs, NB)
                    sp.dma_start(g_dram, wT[:]).then_inc(s_gd, 16)
                    sp.wait_ge(s_gd, 16)

                @block.gpsimd
                def _(pool):
                    norm_pool(pool, m, ns, twice=False)
                    pool.memset(w[:], 1.0).then_inc(s_wg, 1)
                    if gated:
                        pool.memset(yT[:], 0.0)
                    pool.wait_ge(raw_in, 16)
                    if not gated:
                        pool.tensor_tensor(bcol[:, 0], m.raw[:, CH * W:CH * W + CH],
                                           m.one[:].to_broadcast([P, CH]), ALU.mult)
                    for c in range(CH):
                        split(pool, 0, c, 0)

                @block.scalar
                def _(act):
                    norm_act(act, m, ns)
                    act.wait_ge(s_par, 16 * n_par)
                    act.activation(wgh[:], wg[:], ACT.Copy).then_inc(s_wg, 1)
                    act.wait_ge(s_sh, 1)
                    act.activation(ex[:], sh[:], ACT.Exp).then_inc(s_ex, 1)
                    for blk in range(NB):
                        act.wait_ge(s_wt, blk + 1)
                        act.activation(wT[:, blk * BLK:(blk + 1) * BLK], ps[0:E + 1, blk, :], ACT.Copy)\
                            .then_inc(s_wTs, 1)
                    if not gated:
                        for blk in range(NB):
                            for k in range(KD):
                                n = blk * KD + k
                                act.wait_ge(s_b2, n + 1)
                                act.activation(yT[:, k, blk * BLK:(blk + 1) * BLK], ps[:, 4 + n % 4, :],
                                               ACT.Copy).then_inc(s_y0, 1)

                @block.vector
                def _(dve):
                    norm_dve(dve, m, ns)
                    dve.wait_ge(s_wg, 2)
                    dve.tensor_tensor(wgl[:], wg[:], wgh[:].bitcast(FP32), ALU.subtract).then_inc(s_wg, 1)
                    ch = Chain(dve, s_ch)

                    def then(instruction):
                        ch.mark(instruction)
                        ch.wait()

                    def over_j(v):
                        return v.unsqueeze(2).to_broadcast([P, NT, E, E])

                    def over_e(v):
                        return v.unsqueeze(3).to_broadcast([P, NT, E, E])

                    dve.wait_ge(s_lg, 1)
                    then(dve.tensor_tensor(lg[:], ps[:, 4, 0:NT * E].rearrange("p (t e) -> p t e", e=E),
                                           bias[:].unsqueeze(1).to_broadcast([P, NT, E]), ALU.add))
                    dve.reduce_max(mx[:], lg[:], AX.X).then_inc(s_ch, 1)
                    ch.n += 1
                    then(dve.tensor_tensor(gt[:], over_j(lg[:]), over_e(lg[:]), ALU.is_gt))
                    dve.tensor_tensor(sh[:], lg[:], mx[:].unsqueeze(2).to_broadcast([P, NT, E]),
                                      ALU.subtract).then_inc(s_sh, 1)
                    if gated:
                        then(dve.tensor_tensor(eq[:], over_j(lg[:]), over_e(lg[:]), ALU.is_equal))
                        then(dve.tensor_tensor(eq[:], eq[:], tri[:].unsqueeze(1).to_broadcast([P, NT, E, E]),
                                               ALU.mult))
                        then(dve.tensor_tensor(gt[:], gt[:], eq[:], ALU.add))
                    then(dve.reduce_sum(rank[:], gt[:], AX.X))
                    then(dve.tensor_scalar(mk[:], rank[:], float(TOPK0 if gated else TOPK1), None, ALU.is_lt))
                    dve.wait_ge(s_ex, 1)
                    then(dve.tensor_tensor(em[:], ex[:], mk[:], ALU.mult))
                    then(dve.reduce_sum(sm[:], em[:], AX.X))
                    then(dve.reciprocal(rc[:], sm[:]))
                    dve.tensor_tensor(w[:, :, 0:E], em[:], rc[:].unsqueeze(2).to_broadcast([P, NT, E]),
                                      ALU.mult).then_inc(s_w, 1)

                @block.tensor
                def _(pe):
                    norm_pe(pe, m, ns)
                    pe.wait_ge(s_wg, 3)
                    for t in range(NT):
                        if t % TPB == 0:
                            pe.wait_ge(ns.lo, ns.blocks + t // TPB + 1)
                        n = 0
                        for k in range(KD):
                            for st, mo in split_passes((m.uh, m.ul), (wgh, wgl)):
                                i = pe.matmul(ps[:, 4, t * E:(t + 1) * E], st[:, k, t * P:(t + 1) * P],
                                              mo[:, k, :], start=n == 0, stop=n == 5)
                                n += 1
                    i.then_inc(s_lg, 1)
                    pe.wait_ge(s_w, 1)
                    for t in range(NT):
                        i = pe.transpose(ps[0:E + 1, t // TPB, (t % TPB) * P:(t % TPB + 1) * P],
                                         w[:, t, :], m.ident[:, :])
                        if t % TPB == TPB - 1:
                            i.then_inc(s_wt, 1)
                    if not gated:
                        for blk in range(NB):
                            pe.wait_ge(s_wTs, blk + 1)
                            for k in range(KD):
                                n = blk * KD + k
                                if n >= 4:
                                    pe.wait_ge(s_y0, n - 3)
                                pe.matmul(ps[:, 4 + n % 4, :], b2[:, k * P:(k + 1) * P],
                                          wT[0:E, blk * BLK:(blk + 1) * BLK], start=True, stop=True)\
                                    .then_inc(s_b2, 1)

        with ExitStack() as c3:
            def sb3(name, shape, dt=FP32):
                return c3.enter_context(nc.sbuf_tensor(f"{tag}_{name}", shape, dt))

            gates = sb3("gates", [P, 3 if gated else 2, T])
            sa = sb3("sa", [P, 2, BLK])
            tt = sb3("tt", [P, 2, BLK]) if gated else None
            g = sb3("g", [P, 2, BLK])
            hh, hl = (sb3(f"h{n}", [P, 4, BLK], FP32R) for n in "hl")
            s_g = [sem(f"g{n}") for n in range(2)]
            s_gmix = [sem(f"gmix{n}") for n in range(NMIX0)] if gated else None
            s_h, s_sa, s_t, s_gate, s_hh, s_hl, s_out, s_y = (
                sem(n) for n in ("h", "sa", "t", "gate", "hh", "hl", "out", "y"))
            s_yt, s_x = sem("yt"), sem("x")
            last_pair = lay.pairs
            HB = lay.hbanks

            def gate_of(st):
                return 2 - st.chunk if st.mixed else st.group

            with nc.Block() as block:
                @block.sync
                def _(sp):
                    def weights(group, splits_before):
                        sp.wait_ge(s_split, splits_before)
                        if isinstance(group, int) and gated and group == E + 1:
                            sp.dma_start(m.raw[:, 0:NMIX0 * W], a["f0_wmix"]).then_inc(raw_in, 16)
                        else:
                            sp.dma_start(m.raw[:, 0:w_dram.shape[2]], w_dram[group]).then_inc(raw_in, 16)

                    def gate_row(group, par, steps_before):
                        if steps_before is not None:
                            sp.wait_ge(s_gate, steps_before)
                        sp.dma_start(gates[:, par, :], g_dram[group].partition_broadcast(P))\
                            .then_inc(s_g[par], 16)

                    n2 = len(lay.body)
                    gate_row(0, 0, None)
                    weights(1, CH)
                    gate_row(1, 1, None)

                    def pair(i):
                        weights(2 * i, 2 * i * CH)
                        gate_row(2 * i, 0, i * n2 - n2 // 2)
                        weights(2 * i + 1, (2 * i + 1) * CH)
                        gate_row(2 * i + 1, 1, i * n2)

                    with sp.Fori(1, last_pair) as i:
                        pair(i)
                    if not gated:
                        pair(last_pair)
                    else:
                        i = last_pair
                        weights(2 * i, 2 * i * CH)
                        gate_row(2 * i, 0, i * n2 - n2 // 2)
                        weights(2 * i + 1, (2 * i + 1) * CH)
                        for mix in range(NMIX0):
                            par = 2 - mix
                            if mix:
                                sp.wait_ge(s_gate, i * n2 + (mix - 1) * (n2 // 2))
                            for e in range(MIX0):
                                sp.dma_start(gates[e * REM0:(e + 1) * REM0, par, :],
                                             g_dram[mix * MIX0 + e].partition_broadcast(REM0))\
                                    .then_inc(s_gmix[mix], 16)
                            sp.dma_start(gates[MIX0 * REM0:P, par, :],
                                         g_dram[E].partition_broadcast(P - MIX0 * REM0))\
                                .then_inc(s_gmix[mix], 16)

                @block.gpsimd
                def _(pool):
                    def group_split(group, par, chunks, steps_before):
                        pool.wait_ge(raw_in, 16 * group + 16)
                        if steps_before is not None:
                            pool.wait_ge(s_out, steps_before)
                        if not gated:
                            pool.tensor_tensor(bcol[:, par], m.raw[:, CH * W:CH * W + CH],
                                           m.one[:].to_broadcast([P, CH]), ALU.mult)
                        for c in range(chunks):
                            split(pool, group, c, par)

                    half = len(lay.body) // 2
                    group_split(1, 1, CH, None)
                    with pool.Fori(1, last_pair) as i:
                        group_split(2 * i, 0, CH, i * 2 * half - half)
                        group_split(2 * i + 1, 1, CH, i * 2 * half)
                    i = last_pair
                    group_split(2 * i, 0, CH, i * 2 * half - half)
                    group_split(2 * i + 1, 1, NMIX0 if gated else CH, i * 2 * half)

                @block.scalar
                def _(act):
                    def early(st, base):
                        n = base.n + st.n
                        act.wait_ge(s_h, n + 1)
                        if not (base.at_start and st.n < 2):
                            act.wait_ge(s_gate, n - 1)
                        if gated:
                            act.activation(sa[:, st.n % 2], ps[:, 2 * (st.n % 2), :], ACT.Silu)\
                                .then_inc(s_sa, 1)
                        else:
                            if st.blk == 0 and st.chunk == 0:
                                act.wait_ge(s_split, base.chunk + st.group * CH + 1)
                            act.activation(sa[:, st.n % 2], ps[:, st.n % 4, :], ACT.Gelu,
                                           bias=bcol[:, st.group, st.chunk:st.chunk + 1]).then_inc(s_sa, 1)

                    def late(st, base):
                        n = base.n + st.n
                        act.wait_ge(s_gate, n + 1)
                        if not (base.at_start and st.n < 4):
                            act.wait_ge(s_out, n - 3)
                        act.activation(hh[:, st.n % 4], g[:, st.n % 2], ACT.Copy).then_inc(s_hh, 1)

                    walk(lay, act, 1, early, late)

                @block.vector
                def _(dve):
                    def add_out(block, par_block, blk, steps):
                        dve.wait_ge(s_out, steps)
                        bank = 4 + 2 * (par_block % 2)
                        y = yT[:, :, blk * BLK:(blk + 1) * BLK]
                        dve.tensor_tensor(y, y, ps[:, bank:bank + 2, :], ALU.add).then_inc(s_y, 1)

                    def early(st, base):
                        n = base.n + st.n
                        dve.wait_ge(s_sa, n + 1)
                        if st.mixed:
                            if st.blk == 0:
                                dve.wait_ge(s_gmix[st.chunk], 16 * (MIX0 + 1))
                        elif st.blk == 0 and st.chunk == 0:
                            dve.wait_ge(s_g[st.group], base.pair * 16 + 16)
                        src = sa[:, st.n % 2]
                        if gated:
                            dve.tensor_tensor(tt[:, st.n % 2], src, ps[:, 2 * (st.n % 2) + 1, :], ALU.mult)\
                                .then_inc(s_t, 1)
                            dve.wait_ge(s_t, n + 1)
                            src = tt[:, st.n % 2]
                        elif not (base.at_start and st.n < 2):
                            dve.wait_ge(s_hl, n - 1)
                        dve.tensor_tensor(g[:, st.n % 2], src,
                                          gates[:, gate_of(st), st.blk * BLK:(st.blk + 1) * BLK],
                                          ALU.mult).then_inc(s_gate, 1)

                    def late(st, base):
                        n = base.n + st.n
                        dve.wait_ge(s_hh, n + 1)
                        dve.tensor_tensor(hl[:, st.n % 4], g[:, st.n % 2], hh[:, st.n % 4].bitcast(FP32),
                                          ALU.subtract).then_inc(s_hl, 1)
                        if st.chunk == 2 and not (base.at_start and st.block == 0):
                            add_out(base.block + st.block, st.block - 1, (st.blk - 1) % NB,
                                    base.n + st.n - st.chunk)

                    walk(lay, dve, 1, early, late)
                    total = last_pair * len(lay.body) + len(lay.tail)
                    add_out(None, 1, NB - 1, total)
                    for t in range(0, NT, 2):
                        dve.wait_ge(s_yt, t // 2 + 1)
                        xs = m.x[:, t:t + 2, :]
                        dve.tensor_tensor(xs, xs, ps[:, t // 2, :].rearrange("p (t n) -> p t n", t=2),
                                          ALU.add).then_inc(s_x, 1)

                @block.tensor
                def _(pe):
                    def early(st, base):
                        n = base.n + st.n
                        if st.blk == 0:
                            pe.wait_ge(s_split, base.chunk + st.group * CH + st.chunk + 1)
                        if not (base.at_start and st.n < HB):
                            if gated:
                                pe.wait_ge(s_gate, n - 1)
                            else:
                                pe.wait_ge(s_sa, n - 3)
                        for w in range(n_in):
                            bank = 2 * (st.n % 2) + w if gated else st.n % 4
                            q = 0
                            for k in range(KD):
                                col = st.chunk * W + (w * KD + k) * P
                                for sta, mo in split_passes((wh, wl), (m.uh, m.ul)):
                                    i = pe.matmul(ps[:, bank, :], sta[:, st.group, col:col + P],
                                                  mo[:, k, st.blk * BLK:(st.blk + 1) * BLK],
                                                  start=q == 0, stop=q == 5)
                                    q += 1
                        i.then_inc(s_h, 1)

                    def late(st, base):
                        n = base.n + st.n
                        pe.wait_ge(s_hl, n + 1)
                        if st.first and not (base.at_start and st.block < 2):
                            pe.wait_ge(s_y, base.block + st.block - 1)
                        for k in range(KD):
                            bank = 4 + 2 * (st.block % 2) + k
                            col = st.chunk * W + lead_w + k * P
                            for q, (sta, mo) in enumerate(split_passes((wh, wl), (hh, hl))):
                                i = pe.matmul(ps[:, bank, :], sta[:, st.group, col:col + P],
                                              mo[:, st.n % 4, :], start=st.first and q == 0,
                                              stop=st.last and q == 2)
                        i.then_inc(s_out, 1)

                    walk(lay, pe, 2 if gated else 3, early, late)
                    pe.wait_ge(s_y, last_pair * 2 * NB + 2 * NB)
                    for t in range(NT):
                        for k in range(KD):
                            i = pe.transpose(ps[:, t // 2, (t % 2) * D + k * P:(t % 2) * D + (k + 1) * P],
                                             yT[:, k, t * P:(t + 1) * P], m.ident[:, :])
                        if t % 2:
                            i.then_inc(s_yt, 1)



HEADS1 = [(b, h) for b in range(B) for h in range(H1)]
TQ = S // P
NTQ = len(HEADS1) * TQ
NSTK = 2 * (TQ // 4) + 3


class Bank:

    def __init__(self, kind, *at):
        self.kind, self.at = kind, at


class BankOrder:

    def __init__(self):
        self.uses = [Bank("stack", 0, n) for n in range(NSTK)]
        self.step = []
        for g in range(NTQ + 2):
            head, t = divmod(g, TQ)
            now = []
            if g < NTQ:
                now += [Bank("probs", g, part) for part in range(3)]
            if g % 2 == 0 and 2 <= g:
                now.append(Bank("values", g // 2 - 1))
            if g % 2 == 1 and 3 <= g:
                now.append(Bank("project", g // 2 - 1))
            if g < NTQ and head + 1 < len(HEADS1):
                now += [Bank("stack", head + 1, n) for n in {3: (0, 1), 4: (2, 3), 5: (4, 5, 6)}.get(t, ())]
            self.step.append(now)
            self.uses += now
        acts = dves = 0
        self.find = {}
        for k, u in enumerate(self.uses):
            u.k = k
            u.bank = 6 + k % 2
            if u.kind in ("stack", "probs"):
                acts += 1
            else:
                dves += 1
            u.act, u.dve = acts, dves
            self.find[(u.kind, *u.at)] = u

    def wait_free(self, pe, u, s_act, s_dve):
        if u.k >= 2:
            old = self.uses[u.k - 2]
            if old.kind in ("stack", "probs"):
                pe.wait_ge(s_act, old.act)
            else:
                pe.wait_ge(s_dve, old.dve)


def attention1(nc, m, a, raw_in):
    ps = m.ps
    with ExitStack() as ctx:
        def sb(name, shape, dt=FP32):
            return ctx.enter_context(nc.sbuf_tensor(f"b_{name}", shape, dt))

        def sem(name):
            return ctx.enter_context(nc.semaphore(f"b_{name}"))

        NH = len(HEADS1)
        qs = sb("qs", [P, NH, TQ, DH1])
        kvs = sb("kvs", [P, NH, NKT, 2 * DH1])
        woh, wol = (sb(f"wo{n}", [P, H1, D], FP32R) for n in "hl")
        maskm = sb("maskm", [P, B, SCP], FP32R)
        row0 = sb("row0", [P, P], FP32R)
        bo = sb("bo", [P, D])

        with ExitStack() as c2:
            def sb2(name, shape, dt=FP32):
                return c2.enter_context(nc.sbuf_tensor(f"b_{name}", shape, dt))

            wraw = m.raw[:, 0:KD * 3 * D].rearrange("p (k n) -> p k n", k=KD)
            oraw = m.raw[:, KD * 3 * D:KD * 3 * D + H1 * D].rearrange("p (h n) -> p h n", h=H1)
            craw = m.raw[0:HC, 2560:2560 + 4 * D].rearrange("p (k n) -> p k n", k=2)
            wh, wl = (sb2(f"w{n}", [P, KD, 3 * D], FP32R) for n in "hl")
            wch, wcl = (sb2(f"wc{n}", [HC, 2, 2 * D], FP32R) for n in "hl")
            ll_gb = sb2("ll_gb", [P, 2, KD])
            gq, gk = sb2("gq", [P, DH1]), sb2("gk", [P, DH1])
            zf = sb2("zf", [P, KD, BLK])
            sq = sb2("sq", [P, 2, 2 * H1, DH1])
            ss = sb2("ss", [P, 2, 2 * H1])
            r1 = sb2("r1", [P, 2, 2 * H1])
            rr = sb2("rr", [P, 2, 2 * H1])
            half = sb2("half", [P, 2 * H1])
            qk = sb2("qk", [P, 2, 2 * H1, DH1])
            mku = sb2("mku", [1, B, SC], UINT8)
            mkf = sb2("mkf", [1, B, SC])
            ns = m.norm
            s_w, s_par, s_wh, s_wl, s_mk = (sem(n) for n in ("w", "par", "wh", "wl", "mk"))
            s_gq, s_p, s_sq, s_v, s_ss, s_r1, s_r, s_qk, s_g = (
                sem(n) for n in ("gq", "p", "sq", "v", "ss", "r1", "r", "qk", "g"))

            units = [(t, t // TQ, t % TQ) for t in range(NT)] + [(NT + b, b, TQ) for b in range(B)]

            def shape_of(u):
                return (P, 2 * H1) if u < NT else (SCP, H1)

            with nc.Block() as block:
                @block.sync
                def _(sp):
                    sp.dma_start(ll_gb[:], a["ll_gb"]).then_inc(s_par, 16)
                    sp.dma_start(gq[:], a["qn_g"].partition_broadcast(P)).then_inc(s_par, 16)
                    sp.dma_start(gk[:], a["kn_g"].partition_broadcast(P)).then_inc(s_par, 16)
                    sp.dma_start(bo[:], a["bo"].partition_broadcast(P)).then_inc(s_par, 16)
                    sp.dma_start(mku[:], a["mask"].rearrange("(o b) s -> o b s", o=1)).then_inc(s_par, 16)
                    sp.dma_start(wraw, a["wqkv1"]).then_inc(s_w, 16)
                    sp.dma_start(craw, a["wc1"]).then_inc(s_w, 16)
                    for n in range(2):
                        sp.dma_start(oraw[n * DH1:(n + 1) * DH1], a["wo1"]).then_inc(s_w, 16)
                    sp.wait_ge(s_par, 80)

                @block.gpsimd
                def _(pool):
                    pool.memset(half[:], -0.5).then_inc(s_mk, 1)
                    pool.memset(maskm[:].bitcast(FP32), 0.0).then_inc(s_mk, 1)
                    pool.memset(row0[:].bitcast(FP32), 0.0).then_inc(s_mk, 1)
                    norm_pool(pool, m, ns, twice=True)
                    pool.wait_ge(s_wh, 2)
                    pool.tensor_tensor(wl[:], wraw, wh[:].bitcast(FP32), ALU.subtract).then_inc(s_wl, 1)
                    pool.tensor_tensor(wcl[:], craw, wch[:].bitcast(FP32), ALU.subtract).then_inc(s_wl, 1)
                    pool.wait_ge(s_gq, 1)

                    def rms(n):
                        u = units[n][0]
                        rows, w = shape_of(u)
                        sl = n % 2
                        pool.wait_ge(s_ss, n + 1)
                        pool.tensor_scalar(r1[0:rows, sl, 0:w], ss[0:rows, sl, 0:w], 1.0 / DH1, 1e-16,
                                           ALU.mult, ALU.max).then_inc(s_r1, 1)
                        pool.wait_ge(s_r1, n + 1)
                        pool.tensor_tensor(rr[0:rows, sl, 0:w], r1[0:rows, sl, 0:w], half[0:rows, 0:w],
                                           ALU.pow).then_inc(s_r, 1)

                    def gains(n):
                        u, b, t = units[n]
                        rows, w = shape_of(u)
                        hs = slice(b * H1, (b + 1) * H1)
                        pool.wait_ge(s_qk, n + 1)
                        if u < NT:
                            pool.tensor_tensor(qs[:, hs, t, :], qk[:, n % 2, 0:H1],
                                               gq[:].unsqueeze(1).to_broadcast([P, H1, DH1]), ALU.mult)
                        pool.tensor_tensor(kvs[0:rows, hs, t, 0:DH1], qk[0:rows, n % 2, w - H1:w],
                                           gk[0:rows].unsqueeze(1).to_broadcast([rows, H1, DH1]),
                                           ALU.mult).then_inc(s_g, 1)

                    for n in range(len(units)):
                        rms(n)
                        if n:
                            gains(n - 1)
                    gains(len(units) - 1)
                    pool.wait_ge(s_wh, 3)
                    pool.tensor_tensor(wol[:], oraw, woh[:].bitcast(FP32), ALU.subtract).then_inc(s_wl, 1)

                @block.scalar
                def _(act):
                    act.wait_ge(s_w, 64)
                    act.activation(wh[:], wraw, ACT.Copy).then_inc(s_wh, 1)
                    act.activation(wch[:], craw, ACT.Copy).then_inc(s_wh, 1)
                    norm_act(act, m, ns, zf)
                    for n, (u, b, t) in enumerate(units):
                        rows, w = shape_of(u)
                        bank = 4 + 2 * (n % 2)
                        act.wait_ge(s_p, n + 1)
                        if n >= 2:
                            act.wait_ge(s_ss, n - 1)
                        act.activation(sq[0:rows, n % 2, 0:w].rearrange("p h d -> p (h d)"),
                                       ps[0:rows, bank, 0:w * DH1], ACT.Square).then_inc(s_sq, 1)
                        act.activation(kvs[0:rows, b * H1:(b + 1) * H1, t, DH1:2 * DH1],
                                       ps[0:rows, bank + 1, 0:D].rearrange("p (h d) -> p h d", h=H1),
                                       ACT.Copy).then_inc(s_v, 1)
                    act.activation(woh[:], oraw, ACT.Copy).then_inc(s_wh, 1)

                @block.vector
                def _(dve):
                    dve.wait_ge(s_par, 80)
                    dve.tensor_scalar(gq[:], gq[:], float(DH1) ** -0.5, None, ALU.mult).then_inc(s_gq, 1)
                    dve.tensor_copy(mkf[:], mku[:]).then_inc(s_mk, 1)
                    norm_dve(dve, m, ns, ll_gb, zf)
                    dve.wait_ge(s_mk, 4)
                    dve.memset(maskm[0:1, :, SC:SCP].bitcast(FP32), NEG)
                    dve.memset(row0[0:1, :].bitcast(FP32), 1.0)
                    dve.tensor_scalar(maskm[0:1, :, 0:SC], mkf[:], 1.0, -NEG, ALU.subtract, ALU.mult)

                    def squares(n):
                        rows, w = shape_of(units[n][0])
                        dve.wait_ge(s_sq, n + 1)
                        if n >= 2:
                            dve.wait_ge(s_r1, n - 1)
                        dve.reduce_sum(ss[0:rows, n % 2, 0:w], sq[0:rows, n % 2, 0:w], AX.X).then_inc(s_ss, 1)

                    def normed(n):
                        rows, w = shape_of(units[n][0])
                        dve.wait_ge(s_r, n + 1)
                        dve.wait_ge(s_v, n + 1)
                        if n >= 2:
                            dve.wait_ge(s_g, n - 1)
                        dve.tensor_tensor(qk[0:rows, n % 2, 0:w],
                                          ps[0:rows, 4 + 2 * (n % 2), 0:w * DH1]
                                          .rearrange("p (h d) -> p h d", h=w),
                                          rr[0:rows, n % 2, 0:w].unsqueeze(2).to_broadcast([rows, w, DH1]),
                                          ALU.mult).then_inc(s_qk, 1)

                    for n in range(len(units)):
                        squares(n)
                        if n:
                            normed(n - 1)
                    normed(len(units) - 1)

                @block.tensor
                def _(pe):
                    norm_pe(pe, m, ns)
                    pe.wait_ge(s_wl, 2)
                    for n, (u, b, t) in enumerate(units):
                        rows, w = shape_of(u)
                        bank = 4 + 2 * (n % 2)
                        if u < NT:
                            pe.wait_ge(ns.lo, ns.blocks + u // TPB + 1)
                        if n >= 2:
                            pe.wait_ge(s_qk, n - 1)
                            pe.wait_ge(s_v, n - 1)
                        parts_ = ((0, 0, 2 * H1 * DH1), (1, 2 * D, D)) if u < NT else ((0, 0, D), (1, D, D))
                        for bk, col, width in parts_:
                            q = 0
                            for k in range(2):
                                if u < NT:
                                    pairs = split_passes((m.uh, m.ul), (wh, wl))
                                else:
                                    pairs = split_passes((m.cxh, m.cxl), (wch, wcl))
                                for st, mo in pairs:
                                    sta = st[:, k, u * P:(u + 1) * P] if u < NT else st[:, k, b, :]
                                    i = pe.matmul(ps[0:rows, bank + bk, 0:width], sta,
                                                  mo[:, k, col:col + width], start=q == 0, stop=q == 5)
                                    q += 1
                        i.then_inc(s_p, 1)

        order = BankOrder()
        qst = sb("qst", [P, 2, 2, S], FP32R)
        kst = sb("kst", [P, 2, NK1], FP32R)
        vst = sb("vst", [P, 2, NKT, 2 * DH1], FP32R)
        qc = m.z[:, :, :, :].rearrange("p a t d -> p (a t d)").rearrange("p (t w e d) -> p t w e d", t=TQ, w=2, e=2)
        kc = sb("kc", [P, NKT, 2, DH1])
        pth, ptl = (u[:, :, :].rearrange("p k t -> p (k t)").rearrange("p (c n) -> p c n", c=TQ)
                    for u in (m.uh, m.ul))
        pch, pcl = (sb(f"pc{n}", [SCP, BLK], FP32R) for n in "hl")
        nmx, sm, rc = (sb(n, [P, NTQ]) for n in ("nmx", "sm", "rc"))
        raw = sb("raw", [P, 2, NKT, P])
        ex = sb("ex", [P, 2, NK1])
        oh, ol = (sb(f"o{n}", [P, 2 * P], FP32R) for n in "hl")
        s_bo, s_hi2, s_cat, s_vst = (sem(n) for n in ("bo", "cath", "cat", "vst"))
        s_s, s_mx, s_e, s_rc, s_r, s_phi, s_plo, s_dlo, s_oh, s_act, s_dve = (
            sem(n) for n in ("s", "mx", "e", "rc", "bank", "phi", "plo", "dlo", "oh", "act", "dve"))

        def prob_part(g, part, whole, context):
            c = slice((g % 4) * P, (g % 4 + 1) * P)
            return whole[:, 4 * part:4 * part + 4, c] if part < 2 else context[:, c]

        KEY_ROWS = ((P, slice(0, TQ)), (SCP, slice(TQ, NKT)))

        def twice(v):
            return v.unsqueeze(2).to_broadcast([P, TQ, 2, DH1])

        def lower_done(eng, g, part):
            if part == 0:
                eng.wait_ge(s_dlo, g + 1)
            else:
                eng.wait_ge(s_plo, 2 * g + part)

        def raw_part(g, part):
            return raw[:, g % 2, 4 * part:4 * part + 4, :] if part < 2 else raw[0:SCP, g % 2, TQ, :]

        def flat(slot):
            return ps[:, 3 * slot:3 * slot + 3, :].rearrange("p k n -> p (k n)")[:, 0:NK1]

        with nc.Block() as block:
            @block.sync
            def _(sp):
                sp.dma_start(m.raw[:, :], a["f1_w"][0]).then_inc(raw_in, 16)

            @block.gpsimd
            def _(pool):
                def lower_queries(head):
                    pool.wait_ge(s_hi2, 3 * head + 1)
                    pool.tensor_tensor(qc[:, :, 1].bitcast(FP32R), twice(qs[:, head]), qc[:, :, 0],
                                       ALU.subtract).then_inc(s_cat, 1)

                def lower_keys(head):
                    pool.wait_ge(s_hi2, 3 * head + 2)
                    for rows, ts in KEY_ROWS:
                        i = pool.tensor_tensor(kc[0:rows, ts, 1].bitcast(FP32R), kvs[0:rows, head, ts, 0:DH1],
                                               kc[0:rows, ts, 0], ALU.subtract)
                    i.then_inc(s_cat, 1)

                def lower_values(head):
                    pool.wait_ge(s_hi2, 3 * head + 3)
                    vb = vst[:, head % 2]
                    for rows, ts in KEY_ROWS:
                        i = pool.tensor_tensor(vb[0:rows, ts, DH1:2 * DH1], kvs[0:rows, head, ts, DH1:2 * DH1],
                                               vb[0:rows, ts, 0:DH1].bitcast(FP32), ALU.subtract)
                    i.then_inc(s_vst, 1)

                lower_queries(0)
                lower_keys(0)
                lower_values(0)
                pool.tensor_tensor(m.x[:], m.x[:], bo[:].unsqueeze(1).to_broadcast([P, NT, D]), ALU.add)\
                    .then_inc(s_bo, 1)
                for g in range(NTQ):
                    for part in (1, 2):
                        pool.wait_ge(s_phi, 3 * g + part + 1)
                        pool.tensor_tensor(prob_part(g, part, ptl, pcl), raw_part(g, part),
                                           prob_part(g, part, pth, pch).bitcast(FP32), ALU.subtract)\
                            .then_inc(s_plo, 1)
                    head, t = divmod(g, TQ)
                    if head + 1 < NH:
                        if t == 1:
                            lower_queries(head + 1)
                        elif t == 2:
                            lower_keys(head + 1)
                        elif t == 4:
                            lower_values(head + 1)

            @block.scalar
            def _(act):
                def exps(g):
                    act.wait_ge(s_mx, g + 1)
                    if g >= 2:
                        act.wait_ge(s_r, order.find[("probs", g - 2, 2)].k + 1)
                    act.activation(ex[:, g % 2], flat(g % 2), ACT.Exp, bias=nmx[:, g:g + 1],
                                   accum_out=sm[:, g:g + 1]).then_inc(s_e, 1)

                def evacuate(u):
                    act.wait_ge(s_r, u.k + 1)
                    bank = ps[:, u.bank, :]
                    if u.kind == "probs":
                        g, part = u.at
                        if g >= 2:
                            lower_done(act, g - 2, part)
                        src = bank.rearrange("p (c n) -> p c n", c=4) if part < 2 else bank[0:SCP, 0:P]
                        act.activation(raw_part(g, part), src, ACT.Copy).then_inc(s_act, 1)
                    elif u.kind == "values":
                        if u.at[0]:
                            act.wait_ge(s_r, order.find[("project", u.at[0] - 1)].k + 1)
                        act.activation(oh[:], bank[:, 0:2 * P], ACT.Copy).then_inc(s_oh, 1)
                    elif u.kind == "stack":
                        head, n = u.at
                        if head >= 2:
                            act.wait_ge(s_s, (head - 1) * TQ)
                        if n < 4:
                            dst, src = qst[:, head % 2, n % 2, (n // 2) * BLK:(n // 2 + 1) * BLK], bank
                        elif n < 6:
                            dst, src = kst[:, head % 2, (n - 4) * BLK:(n - 3) * BLK], bank
                        else:
                            dst, src = kst[:, head % 2, S:NK1], bank[:, 0:SCP]
                        act.activation(dst, src, ACT.Copy).then_inc(s_act, 1)

                def upper_queries(head):
                    if head:
                        act.wait_ge(s_r, order.find[("stack", head - 1, NSTK - 1)].k + 1)
                    act.activation(qc[:, :, 0].bitcast(FP32R), twice(qs[:, head]), ACT.Copy).then_inc(s_hi2, 1)

                def upper_keys(head):
                    for rows, ts in KEY_ROWS:
                        i = act.activation(kc[0:rows, ts, 0].bitcast(FP32R), kvs[0:rows, head, ts, 0:DH1],
                                           ACT.Copy)
                    i.then_inc(s_hi2, 1)

                def upper_values(head):
                    if head >= 2:
                        act.wait_ge(s_r, order.find[("values", 4 * (head - 2) + 3)].k + 1)
                    for rows, ts in KEY_ROWS:
                        i = act.activation(vst[0:rows, head % 2, ts, 0:DH1],
                                           kvs[0:rows, head, ts, DH1:2 * DH1], ACT.Copy)
                    i.then_inc(s_hi2, 1)

                upper_queries(0)
                upper_keys(0)
                upper_values(0)
                for u in order.uses[:NSTK]:
                    evacuate(u)
                exps(0)
                for g in range(NTQ + 2):
                    if g + 1 < NTQ:
                        exps(g + 1)
                    head, t = divmod(g, TQ)
                    if head + 1 < NH:
                        if t == 0:
                            upper_queries(head + 1)
                        elif t == 1:
                            upper_keys(head + 1)
                        elif t == 3:
                            upper_values(head + 1)
                    for u in order.step[g]:
                        evacuate(u)

            @block.vector
            def _(dve):
                def largest(g):
                    dve.wait_ge(s_s, g + 1)
                    dve.tensor_reduce(nmx[:, g:g + 1], flat(g % 2), AX.X, ALU.max, negate=True)\
                        .then_inc(s_mx, 1)

                def inverse(g):
                    dve.wait_ge(s_e, g + 1)
                    dve.reciprocal(rc[:, g:g + 1], sm[:, g:g + 1]).then_inc(s_rc, 1)

                def evacuate(u):
                    bank = ps[:, u.bank, :]
                    if u.kind == "probs":
                        g, part = u.at
                        dve.wait_ge(s_act, u.act)
                        q = g // 2
                        if q >= 2 and g % 2 == 0 and part == 0:
                            dve.wait_ge(s_r, order.find[("values", q - 2)].k + 1)
                        dve.tensor_copy(prob_part(g, part, pth, pch), raw_part(g, part)).then_inc(s_phi, 1)
                        if part == 1:
                            dve.wait_ge(s_phi, 3 * g + 1)
                            dve.tensor_tensor(prob_part(g, 0, ptl, pcl), raw_part(g, 0),
                                              prob_part(g, 0, pth, pch).bitcast(FP32), ALU.subtract)\
                                .then_inc(s_dlo, 1)
                        if part == 2:
                            inverse(g)
                    elif u.kind == "values":
                        dve.wait_ge(s_oh, u.at[0] + 1)
                        dve.tensor_tensor(ol[:], bank[:, 0:2 * P], oh[:].bitcast(FP32), ALU.subtract)\
                            .then_inc(s_dve, 1)
                    elif u.kind == "project":
                        head, pair = divmod(u.at[0], TQ // 2)
                        t = HEADS1[head][0] * TQ + 2 * pair
                        dve.wait_ge(s_r, u.k + 1)
                        dve.wait_ge(s_rc, 2 * u.at[0] + 2)
                        for j in range(2):
                            g = 2 * u.at[0] + j
                            i = dve.scalar_tensor_tensor(m.x[:, t + j, :], bank[:, j * D:(j + 1) * D],
                                                         rc[:, g:g + 1], m.x[:, t + j, :], ALU.mult, ALU.add)
                        i.then_inc(s_dve, 1)

                largest(0)
                largest(1)
                dve.wait_ge(s_bo, 1)
                for g in range(NTQ + 2):
                    if g + 2 < NTQ:
                        largest(g + 2)
                    for u in order.step[g]:
                        evacuate(u)

            @block.tensor
            def _(pe):
                def scores(g):
                    head, t = divmod(g, TQ)
                    b, sl, c = HEADS1[head][0], g % 2, slice(t * P, (t + 1) * P)
                    if t == 0:
                        pe.wait_ge(s_act, order.find[("stack", head, NSTK - 1)].act)
                    if g >= 2:
                        pe.wait_ge(s_e, g - 1)
                    for w in range(2):
                        for n, (k0, k1) in enumerate(((0, BLK), (BLK, S), (S, NK1))):
                            pe.matmul(ps[:, 3 * sl + n, 0:k1 - k0], qst[:, head % 2, w, c],
                                      kst[:, head % 2, k0:k1], start=w == 0, stop=w == 1 and n < 2)
                    pe.matmul(ps[:, 3 * sl + 2, 0:SCP], row0[:], maskm[:, b, :], start=False, stop=True)\
                        .then_inc(s_s, 1)

                def fill(u):
                    order.wait_free(pe, u, s_act, s_dve)
                    if u.kind == "stack":
                        head, n = u.at
                        if n in (0, 4):
                            pe.wait_ge(s_cat, 2 * head + (1 if n == 0 else 2))
                        if n < 4:
                            for j in range(4):
                                i = pe.transpose(ps[:, u.bank, j * P:(j + 1) * P],
                                                 qc[:, 4 * (n // 2) + j, n % 2].rearrange("p e d -> p (e d)"),
                                                 m.ident[:, :])
                        elif n < 6:
                            for j in range(4):
                                i = pe.transpose(ps[:, u.bank, j * P:(j + 1) * P],
                                                 kc[:, 4 * (n - 4) + j].rearrange("p e d -> p (e d)"),
                                                 m.ident[:, :])
                        else:
                            i = pe.transpose(ps[:, u.bank, 0:SCP],
                                             kc[0:SCP, TQ].rearrange("p e d -> p (e d)"), m.ident[0:SCP, 0:SCP])
                    elif u.kind == "probs":
                        g, part = u.at
                        pe.wait_ge(s_e, g + 1)
                        if part < 2:
                            for j in range(4):
                                k = (4 * part + j) * P
                                i = pe.transpose(ps[:, u.bank, j * P:(j + 1) * P], ex[:, g % 2, k:k + P],
                                                 m.ident[:, :])
                        else:
                            i = pe.transpose(ps[0:SCP, u.bank, 0:P], ex[:, g % 2, S:NK1], m.ident[:, :])
                    elif u.kind == "values":
                        q = u.at[0]
                        head, pair = divmod(q, TQ // 2)
                        c = slice((q % 2) * 2 * P, (q % 2 + 1) * 2 * P)
                        lower_done(pe, 2 * q + 1, 0)
                        lower_done(pe, 2 * q + 1, 2)
                        if pair == 0:
                            pe.wait_ge(s_vst, head + 1)
                        for kt in range(NKT):
                            for w in range(2):
                                if kt < TQ:
                                    mo = (pth, ptl)[w][:, kt, c]
                                    sta = vst[:, head % 2, kt, :]
                                else:
                                    mo = (pch, pcl)[w][:, c]
                                    sta = vst[0:SCP, head % 2, kt, :]
                                i = pe.matmul(ps[:, u.bank, 0:2 * P], sta, mo,
                                              start=kt == 0 and w == 0, stop=kt == NKT - 1 and w == 1)
                    else:
                        q = u.at[0]
                        h = HEADS1[q // (TQ // 2)][1]
                        pe.wait_ge(s_dve, order.find[("values", q)].dve)
                        for j in range(2):
                            for n, (st, mo) in enumerate(split_passes((oh, ol), (woh, wol))):
                                i = pe.matmul(ps[:, u.bank, j * D:(j + 1) * D], st[:, j * P:(j + 1) * P],
                                              mo[:, h, :], start=n == 0, stop=n == 2)
                    i.then_inc(s_r, 1)

                for u in order.uses[:NSTK]:
                    fill(u)
                scores(0)
                scores(1)
                for g in range(NTQ + 2):
                    if g + 2 < NTQ:
                        scores(g + 2)
                    for u in order.step[g]:
                        fill(u)


def store_out(nc, m, a, out):
    with ExitStack() as ctx:
        s_out = ctx.enter_context(nc.semaphore("s_out"))
        with nc.Block() as block:
            @block.sync
            def _(sp):
                sp.dma_start(out.rearrange("b (t p) d -> p (b t) d", p=P), m.x[:]).then_inc(s_out, 16)
                sp.wait_ge(s_out, 16)


def program(nc, a, out):
    with ExitStack() as ctx:
        m = Memory(nc, ctx)
        raw0 = ctx.enter_context(nc.semaphore("f0_raw"))
        attention0(nc, m, a, raw0)
        m.norm.next(twice=True, affine=True)
        experts(nc, m, a, "f0", Layer(True, CH0, E // 2, [CH0, NMIX0]), raw0)
        m.norm.next(twice=False, affine=False)
        raw1 = ctx.enter_context(nc.semaphore("f1_raw"))
        attention1(nc, m, a, raw1)
        m.norm.next(twice=True, affine=True)
        experts(nc, m, a, "f1", Layer(False, CH1, E // 2 - 1, [CH1, CH1]), raw1)
        store_out(nc, m, a, out)


def kernel(**inputs):
    import numpy as np
    import concourse.bacc as bacc
    from concourse.bass_utils import run_bass_kernel_spmd

    v = {k: np.asarray(x) for k, x in inputs.items()}
    arrays = {}

    def parts(w, rows=P):
        return w.reshape(-1, rows, w.shape[-1]).transpose(1, 0, 2)

    def vec(g, rows=P):
        return g.reshape(-1, rows).T

    arrays["x"] = v["x"]
    arrays["ctx_768"] = v["ctx_768"]
    arrays["wqo0"] = np.stack([parts(v["L0_xattn_W_Q"]), parts(v["L0_xattn_W_O"])], 1)
    arrays["wkv0"] = np.stack([parts(v["L0_xattn_W_K"], HC), parts(v["L0_xattn_W_V"], HC)], 1)
    arrays["lat_gb"] = np.stack([vec(v["L0_xattn_ln_lat_g"]), vec(v["L0_xattn_ln_lat_b"])], 1)
    arrays["in_gb"] = np.stack([vec(v["L0_xattn_ln_in_g"], HC), vec(v["L0_xattn_ln_in_b"], HC)], 1)
    arrays["lx_gb"] = np.stack([vec(v["L1_xattn_ln_x_g"], HC), vec(v["L1_xattn_ln_x_b"], HC)], 1)
    arrays["c_ident"] = np.eye(P, dtype=np.float32)
    r = np.arange(NC0 * P)
    bd = (r[:, None] // SC == np.arange(D)[None, :] // DH0) & (r[:, None] < KC0)
    arrays["c_bd"] = bd.astype(np.float32).reshape(NC0, P, D).transpose(1, 0, 2)

    w1, w2 = (np.concatenate([v[f"L0_ffn_{n}"], v[f"L0_ffn_{s}"][None]]) for n, s in (("W1", "Ws1"), ("W2", "Ws2")))
    w3 = np.concatenate([v["L0_ffn_W3"], v["L0_ffn_Ws3"][None]]).transpose(0, 2, 1)
    full = CH0 * P

    def chunked_in(w, n):
        return w.reshape(-1, n, P, KD, P).transpose(0, 4, 1, 3, 2).reshape(-1, P, n, KD * P)

    def chunked_out(w, n):
        return w.reshape(-1, n, P, D).transpose(0, 2, 1, 3)

    def packed(ws, n):
        return np.concatenate([chunked_in(w, n) for w in ws[:-1]] + [chunked_out(ws[-1], n)], -1)\
            .reshape(-1, P, n * (len(ws) * 2 * P))

    arrays["f0_w"] = packed([w[:, :full] for w in (w1, w2, w3)], CH0)
    rests = []
    for w in (w1, w2, w3):
        r = w[:, full:].reshape(NMIX0, MIX0 * REM0, D)
        rests.append(np.concatenate([r, np.zeros((NMIX0, P - MIX0 * REM0, D), np.float32)], 1)
                     .reshape(1, NMIX0 * P, D))
    arrays["f0_wmix"] = packed(rests, NMIX0)[0]
    arrays["f0_wg"] = parts(v["L0_ffn_Wg"].T)
    arrays["f0_bias"] = v["L0_ffn_routing_bias"]
    j, e = np.arange(E)[None, :], np.arange(E)[:, None]
    arrays["c_tri"] = (j < e).astype(np.float32)
    arrays["wqkv1"] = parts(np.concatenate([v["L1_xattn_Wq"], v["L1_xattn_Wlkv"]]).T)
    arrays["wc1"] = parts(v["L1_xattn_Wkv"].T, HC)
    arrays["wo1"] = parts(v["L1_xattn_Wo"].T, DH1)
    arrays["ll_gb"] = np.stack([vec(v["L1_xattn_ln_l_g"]), vec(v["L1_xattn_ln_l_b"])], 1)
    arrays["qn_g"], arrays["kn_g"], arrays["bo"] = v["L1_xattn_qn_g"], v["L1_xattn_kn_g"], v["L1_xattn_bo"]
    arrays["mask"] = v["mask_BxS2_bk0"]
    arrays["f1_w"] = np.concatenate([
        packed([v["L1_ffn_W1"].transpose(0, 2, 1), v["L1_ffn_W2"]], CH1),
        v["L1_ffn_b1"].reshape(E, CH1, P).transpose(0, 2, 1)], -1)
    arrays["f1_wg"] = parts(v["L1_ffn_Wr"])
    arrays["f1_bias"] = v["L1_ffn_br"]
    arrays["f1_b2"] = v["L1_ffn_b2"]

    nc = bacc.Bacc("TRN2", target_bir_lowering=False, num_devices=1)
    arrays = {"in_" + k: np.ascontiguousarray(x) for k, x in arrays.items()}
    a = {k[3:]: nc.dram_tensor(k, x.shape, mybir.dt.from_np(x.dtype), kind="ExternalInput").ap()
         for k, x in arrays.items()}
    out = nc.dram_tensor("out_0", (B, S, D), FP32, kind="ExternalOutput").ap()
    program(nc, a, out)
    r = run_bass_kernel_spmd(nc, [arrays], core_ids=[0])
    return r.results[0]["out_0"]
```

```python
import concourse.bass as bass
from concourse import mybir
from contextlib import ExitStack

FP32 = mybir.dt.float32
FP32R = mybir.dt.float32r
UINT8 = mybir.dt.uint8
ALU = mybir.AluOpType
ACT = mybir.ActivationFunctionType
AX = mybir.AxisListType

P = 128
B, S, D = 2, 1024, 256
T = B * S
NT = T // P
KD = D // P
BLK = 512
NB = T // BLK
TPB = BLK // P
SC, DC = 77, 192
HC = DC // 2
EPS = 1e-5
H0 = 8
DH0 = D // H0
G0 = P // DH0
KC0 = H0 * SC
NC0 = -(-KC0 // P)
E = 8
H_FF0 = D * 2 * 4 // 3
CH0 = H_FF0 // P
REM0 = H_FF0 - CH0 * P
MIX0 = P // REM0
NMIX0 = (E + 1) // MIX0
TOPK0 = 4
H1 = 4
DH1 = D // H1
SCP = SC + 1
NKT = S // P + 1
NK1 = S + SCP
NEG = -(2.0 - 2.0 ** -11) * 2.0 ** 127
H_FF1 = 1024
CH1 = H_FF1 // P
TOPK1 = 2


def split_passes(hi_lo_stationary, hi_lo_moving):
    (sh, sl), (mh, ml) = hi_lo_stationary, hi_lo_moving
    return ((sh, mh), (sh, ml), (sl, mh))


class Chain:

    def __init__(self, eng, sem, n=0):
        self.eng, self.sem, self.n = eng, sem, n

    def mark(self, instruction):
        instruction.then_inc(self.sem, 1)
        self.n += 1

    def wait(self):
        self.eng.wait_ge(self.sem, self.n)


class Memory:

    def __init__(self, nc, ctx):
        def sb(name, shape, dt=FP32):
            return ctx.enter_context(nc.sbuf_tensor(name, shape, dt))

        self.ps = ctx.enter_context(nc.psum_tensor("ps", [P, 8, BLK], FP32))
        self.x = sb("x_resid", [P, NT, D])
        self.ident = sb("ident", [P, P])
        self.uh = sb("uh", [P, KD, T], FP32R)
        self.ul = sb("ul", [P, KD, T], FP32R)
        self.z = sb("z", [P, 2, TPB, D])
        self.st = sb("st", [P, NT, 6])
        self.mv = sb("mv", [P, NT, 2])
        self.rs = sb("rs", [P, 4, NT])
        self.mhalf = sb("mhalf", [P, NT])
        self.one = sb("one", [P, 1])
        self.cxh = sb("cxh", [HC, 2, B, SCP], FP32R)
        self.cxl = sb("cxl", [HC, 2, B, SCP], FP32R)
        self.norm = NormSems(nc, ctx)
        self.raw = sb("raw", [P, CH1 * 4 * P + CH1])


class NormSems:

    def __init__(self, nc, ctx):
        def sem(name):
            return ctx.enter_context(nc.semaphore(f"norm_{name}"))

        self.blocks = self.affine_blocks = self.pool_marks = 0

        self.var = sem("var")
        self.rs = sem("rs")
        self.z = sem("z")
        self.zt = sem("zt")
        self.zf = sem("zf")
        self.hi = sem("hi")
        self.lo = sem("lo")
        self.dch = sem("dch")
        self.pch = sem("pch")

    def next(self, twice, affine):
        self.blocks += NB
        self.affine_blocks += NB * affine
        self.pool_marks += NB * (6 if twice else 1)



def norm_dve(dve, m, s, affine=None, zf=None):
    n0, a0 = s.blocks, s.affine_blocks
    ch = Chain(dve, s.dch, n0 * TPB)
    for blk in range(NB):
        for j in range(TPB):
            t = blk * TPB + j
            ch.mark(dve.bn_stats(m.st[:, t, :], m.x[:, t, :]))
        ch.wait()
        for j in range(TPB):
            t = blk * TPB + j
            i = dve.bn_aggr(m.mv[:, t, :], m.st[:, t, :])
        i.then_inc(s.var, 1)

    def normalise(blk):
        dve.wait_ge(s.rs, n0 + blk + 1)
        if blk >= 2:
            dve.wait_ge(s.zt, n0 + blk - 1)
        for j in range(TPB):
            t = blk * TPB + j
            i = dve.tensor_scalar(m.z[:, blk % 2, j, :], m.x[:, t, :], m.mv[:, t, 0:1],
                                  m.rs[:, 3, t:t + 1], ALU.subtract, ALU.mult)
        i.then_inc(s.z, 1)

    def lower_half(blk):
        bank = 2 * (blk % 2)
        cols = slice(blk * BLK, (blk + 1) * BLK)
        src = m.ps[:, bank:bank + KD, :]
        if affine is not None:
            dve.wait_ge(s.zt, n0 + blk + 1)
            if blk:
                dve.wait_ge(s.lo, n0 + blk)
            for k in range(KD):
                i = dve.tensor_scalar(zf[:, k, :], m.ps[:, bank + k, :], affine[:, 0, k:k + 1],
                                      affine[:, 1, k:k + 1], ALU.mult, ALU.add)
            i.then_inc(s.zf, 1)
            src = zf[:, :, :]
        dve.wait_ge(s.hi, n0 + blk + 1)
        dve.tensor_tensor(m.ul[:, :, cols], src, m.uh[:, :, cols].bitcast(FP32),
                          ALU.subtract).then_inc(s.lo, 1)

    normalise(0)
    for blk in range(NB):
        if blk + 1 < NB:
            normalise(blk + 1)
        lower_half(blk)


def norm_pool(pool, m, s, twice):
    n0 = s.blocks
    ch = Chain(pool, s.pch, s.pool_marks)
    for blk in range(NB):
        c = slice(blk * TPB, (blk + 1) * TPB)
        var, half = m.mv[:, c, 1], m.mhalf[:, c]
        tmp, r1, tmp2, r = (m.rs[:, n, c] for n in range(4))
        pool.wait_ge(s.var, n0 + blk + 1)
        ch.mark(pool.tensor_scalar(tmp, var, EPS, None, ALU.add))
        ch.wait()
        if not twice:
            pool.tensor_tensor(r, tmp, half, ALU.pow).then_inc(s.rs, 1)
            continue
        ch.mark(pool.tensor_tensor(r1, tmp, half, ALU.pow))
        ch.wait()
        ch.mark(pool.tensor_tensor(tmp, r1, r1, ALU.mult))
        ch.wait()
        ch.mark(pool.tensor_tensor(tmp2, tmp, var, ALU.mult))
        ch.wait()
        ch.mark(pool.tensor_scalar(tmp, tmp2, EPS, None, ALU.add))
        ch.wait()
        ch.mark(pool.tensor_tensor(tmp2, tmp, half, ALU.pow))
        ch.wait()
        pool.tensor_tensor(r, tmp2, r1, ALU.mult).then_inc(s.rs, 1)


def norm_pe(pe, m, s):
    n0 = s.blocks
    for blk in range(NB):
        bank = 2 * (blk % 2)
        pe.wait_ge(s.z, n0 + blk + 1)
        if blk >= 2:
            pe.wait_ge(s.lo, n0 + blk - 1)
        for k in range(KD):
            for j in range(TPB):
                i = pe.transpose(m.ps[:, bank + k, j * P:(j + 1) * P],
                                 m.z[:, blk % 2, j, k * P:(k + 1) * P], m.ident[:, :])
        i.then_inc(s.zt, 1)


def norm_act(act, m, s, zf=None):
    n0, a0 = s.blocks, s.affine_blocks
    for blk in range(NB):
        bank = 2 * (blk % 2)
        cols = slice(blk * BLK, (blk + 1) * BLK)
        if zf is None:
            act.wait_ge(s.zt, n0 + blk + 1)
            act.activation(m.uh[:, :, cols], m.ps[:, bank:bank + KD, :], ACT.Copy).then_inc(s.hi, 1)
        else:
            act.wait_ge(s.zf, a0 + blk + 1)
            act.activation(m.uh[:, :, cols], zf[:, :, :], ACT.Copy).then_inc(s.hi, 1)



def attention0(nc, m, a, raw_in):
    ps = m.ps
    with ExitStack() as ctx:
        def sb(name, shape, dt=FP32):
            return ctx.enter_context(nc.sbuf_tensor(name, shape, dt))

        def sem(name):
            return ctx.enter_context(nc.semaphore(name))

        wqh, wql = (sb(f"wq0{n}", [P, KD, D], FP32R) for n in "hl")
        woh, wol = (sb(f"wo0{n}", [P, KD, D], FP32R) for n in "hl")
        kbh, kbl = (sb(f"kb0{n}", [P, B, KD, G0, SC], FP32R) for n in "hl")
        vbh, vbl = (sb(f"vb0{n}", [P, B, NC0, D], FP32R) for n in "hl")
        lat_gb = sb("lat_gb", [P, 2, KD])

        with ExitStack() as c2:
            def sb2(name, shape, dt=FP32):
                return c2.enter_context(nc.sbuf_tensor(name, shape, dt))

            wraw = m.raw[:, 0:4 * D].rearrange("p (w k n) -> p w k n", w=2, k=KD)
            craw = sb2("craw", [HC, 2, 2, D])
            wkh, wkl = (sb2(f"wkv0{n}", [HC, 2, 2, D], FP32R) for n in "hl")
            cx = sb2("cx", [SC, B, DC])
            cn = sb2("cn", [SC, B, DC])
            cst = sb2("cst", [SC, B, 6])
            cmv = sb2("cmv", [SC, B, 2])
            crs = sb2("crs", [SC, 2, B])
            in_gb = sb2("in_gb", [HC, 2, 2])
            lx_gb = sb2("lx_gb", [HC, 2, 2])
            cf = sb2("cf", [HC, 2, 2, B, SC])
            c0h, c0l = (sb2(f"c0{n}", [HC, 2, B, SC], FP32R) for n in "hl")
            reph, repl = (sb2(f"rep{n}", [HC, 2, B, NC0 * P], FP32R) for n in "hl")
            bd = sb2("bd", [P, NC0, D])
            vf = sb2("vf", [P, B, NC0, D])

            s_cx, s_par, s_w, s_xl = sem("a0_cx"), sem("a0_par"), sem("a0_w"), sem("a0_xl")
            s_var, s_rs, s_cn, s_ct = sem("a0_var"), sem("a0_rs"), sem("a0_cn"), sem("a0_ct")
            s_cf, s_ch, s_cl, s_rep = sem("a0_cf"), sem("a0_ch"), sem("a0_cl"), sem("a0_rep")
            s_zero, s_wh, s_wl = sem("a0_zero"), sem("a0_wh"), sem("a0_wl")
            s_kt, s_kh, s_kl = sem("a0_kt"), sem("a0_kh"), sem("a0_kl")
            s_v, s_vf, s_vh, s_vl = sem("a0_v"), sem("a0_vf"), sem("a0_vh"), sem("a0_vl")
            s_pch = sem("a0_pch")

            with nc.Block() as block:
                @block.sync
                def _(sp):
                    sp.dma_start(cx[:], a["ctx_768"].rearrange("b s d -> s b d")).then_inc(s_cx, 16)
                    sp.dma_start(m.ident[:], a["c_ident"]).then_inc(s_cx, 16)
                    sp.dma_start(in_gb[:], a["in_gb"]).then_inc(s_par, 16)
                    sp.dma_start(lx_gb[:], a["lx_gb"]).then_inc(s_par, 16)
                    sp.dma_start(craw[:], a["wkv0"]).then_inc(s_w, 16)
                    sp.dma_start(bd[:], a["c_bd"]).then_inc(s_par, 16)
                    sp.dma_start(lat_gb[:], a["lat_gb"]).then_inc(s_par, 16)
                    xv = a["x"].rearrange("b (t p) d -> p (b t) d", p=P)
                    for blk in range(NB):
                        c = slice(blk * TPB, (blk + 1) * TPB)
                        sp.dma_start(m.x[:, c, :], xv[:, c, :]).then_inc(s_xl, 16)
                    sp.wait_ge(s_xl, 16 * NB)

                @block.gpsimd
                def _(pool):
                    ch = Chain(pool, s_pch)
                    pool.memset(m.mhalf[:], -0.5).then_inc(s_zero, 1)
                    pool.memset(m.one[:], 1.0)
                    for t in (m.cxh, m.cxl, reph, repl, kbh, kbl):
                        pool.memset(t[:].bitcast(FP32), 0.0).then_inc(s_zero, 1)
                    pool.wait_ge(s_var, 1)
                    pool.wait_ge(s_zero, 1)
                    ch.mark(pool.tensor_scalar(crs[:, 0, :], cmv[:, :, 1], EPS, None, ALU.add))
                    ch.wait()
                    pool.tensor_tensor(crs[:, 1, :], crs[:, 0, :], m.mhalf[0:SC, 0:B], ALU.pow)\
                        .then_inc(s_rs, 1)
                    pool.wait_ge(s_w, 32)
                    pool.wait_ge(s_wh, 1)
                    pool.tensor_tensor(wkl[:], craw[:], wkh[:].bitcast(FP32), ALU.subtract).then_inc(s_wl, 1)
                    pool.wait_ge(s_wh, 3)
                    pool.tensor_tensor(wql[:], wraw[:, 0], wqh[:].bitcast(FP32), ALU.subtract).then_inc(s_wl, 1)
                    pool.tensor_tensor(wol[:], wraw[:, 1], woh[:].bitcast(FP32), ALU.subtract).then_inc(s_wl, 1)

                @block.scalar
                def _(act):
                    act.dma_start(wraw, a["wqo0"]).then_inc(s_w, 16)
                    act.wait_ge(s_w, 32)
                    act.activation(wkh[:], craw[:], ACT.Copy).then_inc(s_wh, 1)
                    act.wait_ge(s_cf, 1)
                    act.activation(c0h[:], cf[:, 0], ACT.Copy).then_inc(s_ch, 1)
                    act.wait_ge(s_cf, 2)
                    act.wait_ge(s_zero, 3)
                    act.activation(m.cxh[:, :, :, 0:SC], cf[:, 1], ACT.Copy).then_inc(s_ch, 1)
                    act.activation(wqh[:], wraw[:, 0], ACT.Copy).then_inc(s_wh, 1)
                    act.activation(woh[:], wraw[:, 1], ACT.Copy).then_inc(s_wh, 1)
                    act.wait_ge(s_kt, 1)
                    act.wait_ge(s_zero, 7)
                    for g in range(KD):
                        for j in range(G0):
                            r = slice(j * DH0, (j + 1) * DH0)
                            act.activation(kbh[r, :, g, j, :],
                                           ps[r, 1, g * B * SC:(g + 1) * B * SC]
                                           .rearrange("p (b k) -> p b k", b=B), ACT.Copy).then_inc(s_kh, 1)
                    for b in range(B):
                        act.wait_ge(s_vf, b + 1)
                        act.activation(vbh[:, b], vf[:, b], ACT.Copy).then_inc(s_vh, 1)

                @block.vector
                def _(dve):
                    dve.wait_ge(s_cx, 32)
                    for b in range(B):
                        dve.bn_stats(cst[:, b, :], cx[:, b, :]).then_inc(s_cn, 1)
                    dve.wait_ge(s_cn, 2)
                    for b in range(B):
                        i = dve.bn_aggr(cmv[:, b, :], cst[:, b, :])
                    i.then_inc(s_var, 1)
                    dve.wait_ge(s_rs, 1)
                    for b in range(B):
                        dve.tensor_scalar(cn[:, b, :], cx[:, b, :], cmv[:, b, 0:1], crs[:, 1, b:b + 1],
                                          ALU.subtract, ALU.mult).then_inc(s_cn, 1)
                    dve.wait_ge(s_ct, 1)
                    dve.wait_ge(s_par, 64)
                    for w, gb in enumerate((in_gb, lx_gb)):
                        for k in range(2):
                            i = dve.tensor_scalar(cf[:, w, k].rearrange("p b s -> p (b s)"),
                                                  ps[0:HC, 0, k * B * SC:(k + 1) * B * SC],
                                                  gb[:, 0, k:k + 1], gb[:, 1, k:k + 1], ALU.mult, ALU.add)
                        i.then_inc(s_cf, 1)
                    dve.wait_ge(s_ch, 1)
                    dve.tensor_tensor(c0l[:], cf[:, 0], c0h[:].bitcast(FP32), ALU.subtract).then_inc(s_cl, 1)
                    dve.wait_ge(s_ch, 2)
                    dve.wait_ge(s_zero, 5)
                    dve.tensor_tensor(m.cxl[:, :, :, 0:SC], cf[:, 1], m.cxh[:, :, :, 0:SC].bitcast(FP32),
                                      ALU.subtract).then_inc(s_cl, 1)
                    dve.wait_ge(s_cl, 1)
                    for src, dst in ((c0h, reph), (c0l, repl)):
                        for k in range(2):
                            for b in range(B):
                                dve.tensor_copy(dst[:, k, b, 0:KC0].rearrange("p (h s) -> p h s", h=H0),
                                                src[:, k, b:b + 1, :].to_broadcast([HC, H0, SC])
                                                .bitcast(FP32)).then_inc(s_rep, 1)
                    dve.wait_ge(s_kh, KD * G0)
                    for g in range(KD):
                        for j in range(G0):
                            r = slice(j * DH0, (j + 1) * DH0)
                            dve.tensor_tensor(kbl[r, :, g, j, :],
                                              ps[r, 1, g * B * SC:(g + 1) * B * SC]
                                              .rearrange("p (b k) -> p b k", b=B),
                                              kbh[r, :, g, j, :].bitcast(FP32), ALU.subtract).then_inc(s_kl, 1)
                    psv = ps[:, 2:7, :].rearrange("p k n -> p (k n)")
                    dve.wait_ge(s_v, B)
                    for b in range(B):
                        dve.tensor_tensor(vf[:, b].rearrange("p c n -> p (c n)"),
                                          psv[:, b * NC0 * D:(b + 1) * NC0 * D],
                                          bd[:].rearrange("p c n -> p (c n)"), ALU.mult).then_inc(s_vf, 1)
                    for b in range(B):
                        dve.wait_ge(s_vf, b + 1)
                        dve.wait_ge(s_vh, b + 1)
                        dve.tensor_tensor(vbl[:, b], vf[:, b], vbh[:, b].bitcast(FP32),
                                          ALU.subtract).then_inc(s_vl, 1)

                @block.tensor
                def _(pe):
                    pe.wait_ge(s_cx, 32)
                    pe.wait_ge(s_cn, 4)
                    for k in range(2):
                        for b in range(B):
                            o = (k * B + b) * SC
                            i = pe.transpose(ps[0:HC, 0, o:o + SC], cn[:, b, k * HC:(k + 1) * HC],
                                             m.ident[0:SC, 0:SC])
                    i.then_inc(s_ct, 1)
                    pe.wait_ge(s_wl, 1)
                    pe.wait_ge(s_cl, 1)
                    for g in range(KD):
                        n = 0
                        for k in range(2):
                            for st, mo in split_passes((wkh, wkl), (c0h, c0l)):
                                i = pe.matmul(ps[:, 1, g * B * SC:(g + 1) * B * SC],
                                              st[:, 0, k, g * P:(g + 1) * P],
                                              mo[:, k].rearrange("p b s -> p (b s)"),
                                              start=n == 0, stop=n == 5)
                                n += 1
                    i.then_inc(s_kt, 1)
                    pe.wait_ge(s_rep, 8)
                    for b in range(B):
                        for c in range(NC0):
                            u = b * NC0 + c
                            n = 0
                            for k in range(2):
                                for st, mo in split_passes((reph, repl), (wkh, wkl)):
                                    i = pe.matmul(ps[:, 2 + u // 2, (u % 2) * D:(u % 2 + 1) * D],
                                                  st[:, k, b, c * P:(c + 1) * P], mo[:, 1, k, :],
                                                  start=n == 0, stop=n == 5)
                                    n += 1
                        i.then_inc(s_v, 1)

        qh, ql = (sb(f"q0{n}", [P, KD, T], FP32R) for n in "hl")
        zf = sb("zf", [P, KD, BLK])
        mx = sb("mx", [P, 2, H0])
        sm = sb("sm", [P, 2, H0])
        rc = sb("rc", [P, 2, H0])
        sd = sb("sd", [P, 2, H0, SC])
        ex = sb("ex", [P, 2, H0, SC])
        pn = sb("pn", [P, 2, KC0])
        pth, ptl = (sb(f"pt{n}", [P, NC0, BLK], FP32R) for n in "hl")
        oh, ol = (sb(f"o0{n}", [P, KD, BLK], FP32R) for n in "hl")
        ns = m.norm
        s_q, s_qh, s_ql = sem("a_q"), sem("a_qh"), sem("a_ql")
        s_s, s_mx, s_sd, s_e, s_sum, s_rc, s_pn = (sem(f"a_{n}") for n in ("s", "mx", "sd", "e", "sum", "rc", "pn"))
        s_pt, s_pth, s_ptl = sem("a_pt"), sem("a_pth"), sem("a_ptl")
        s_o, s_oh, s_ol, s_y, s_x = (sem(f"a_{n}") for n in ("o", "oh", "ol", "y", "x"))
        scale = float(DH0) ** -0.5
        last_rows = KC0 - (NC0 - 1) * P
        halves = [(0, 3), (2, 5)]

        def tiles():
            return [(t // TPB, t % TPB, t) for t in range(NT)]

        with nc.Block() as block:
            @block.sync
            def _(sp):
                sp.dma_start(m.raw[:, 0:CH0 * 6 * P], a["f0_w"][0]).then_inc(raw_in, 16)

            @block.gpsimd
            def _(pool):
                norm_pool(pool, m, ns, twice=True)
                for blk, j, t in tiles():
                    pool.wait_ge(s_rc, t + 1)
                    if t >= 2:
                        pool.wait_ge(s_pt, t - 1)
                    pool.tensor_tensor(pn[:, t % 2].rearrange("p (h s) -> p h s", h=H0), ex[:, t % 2],
                                       rc[:, t % 2].unsqueeze(2).to_broadcast([P, H0, SC]),
                                       ALU.mult).then_inc(s_pn, 1)

            @block.scalar
            def _(act):
                norm_act(act, m, ns, zf)
                for n in range(NB * KD):
                    blk, g = n // KD, n % KD
                    act.wait_ge(s_q, n + 1)
                    act.activation(qh[:, g, blk * BLK:(blk + 1) * BLK], ps[:, 4 + n % 4, :], ACT.Copy)\
                        .then_inc(s_qh, 1)

                def exps(t):
                    act.wait_ge(s_sd, t + 1)
                    if t >= 2:
                        act.wait_ge(s_pn, t - 1)
                    act.activation(ex[:, t % 2], sd[:, t % 2], ACT.Exp, scale=scale).then_inc(s_e, 1)

                exps(0)
                for blk, j, t in tiles():
                    if t + 1 < NT:
                        exps(t + 1)
                    act.wait_ge(s_pt, t + 1)
                    if j == 0 and blk:
                        act.wait_ge(s_o, blk)
                    c = slice(j * P, (j + 1) * P)
                    act.activation(pth[:, 0:4, c], ps[:, 4, :].rearrange("p (c n) -> p c n", c=4), ACT.Copy)
                    act.activation(pth[0:last_rows, 4, c], ps[0:last_rows, 5, 0:P], ACT.Copy).then_inc(s_pth, 1)
                    if j == TPB - 1:
                        act.wait_ge(s_o, blk + 1)
                        if blk:
                            act.wait_ge(s_y, 2 * blk)
                        act.activation(oh[:], ps[:, 6:8, :], ACT.Copy).then_inc(s_oh, 1)

            @block.vector
            def _(dve):
                norm_dve(dve, m, ns, lat_gb, zf)
                for n in range(NB * KD):
                    blk, g = n // KD, n % KD
                    c = slice(blk * BLK, (blk + 1) * BLK)
                    dve.wait_ge(s_qh, n + 1)
                    dve.tensor_tensor(ql[:, g, c], ps[:, 4 + n % 4, :], qh[:, g, c].bitcast(FP32),
                                      ALU.subtract).then_inc(s_ql, 1)

                def shift(t):
                    sl = 2 * (t % 2)
                    sv = ps[:, sl:sl + 2, 0:G0 * SC].rearrange("p g (h s) -> p g h s", h=G0)
                    dve.wait_ge(s_s, t + 1)
                    dve.reduce_max(mx[:, t % 2].rearrange("p (g h) -> p g h", g=KD), sv, AX.X)\
                        .then_inc(s_mx, 1)
                    dve.wait_ge(s_mx, t + 1)
                    if t >= 2:
                        dve.wait_ge(s_e, t - 1)
                    for g in range(KD):
                        i = dve.tensor_tensor(sd[:, t % 2, g * G0:(g + 1) * G0, :], sv[:, g],
                                              mx[:, t % 2, g * G0:(g + 1) * G0].unsqueeze(2)
                                              .to_broadcast([P, G0, SC]), ALU.subtract)
                    i.then_inc(s_sd, 1)

                def sums(t):
                    dve.wait_ge(s_e, t + 1)
                    dve.reduce_sum(sm[:, t % 2], ex[:, t % 2], AX.X).then_inc(s_sum, 1)
                    dve.wait_ge(s_sum, t + 1)
                    if t >= 2:
                        dve.wait_ge(s_pn, t - 1)
                    dve.reciprocal(rc[:, t % 2], sm[:, t % 2]).then_inc(s_rc, 1)

                shift(0)
                for blk, j, t in tiles():
                    if t + 1 < NT:
                        shift(t + 1)
                    if t == 0:
                        sums(0)
                    if t + 1 < NT:
                        sums(t + 1)
                    dve.wait_ge(s_pth, t + 1)
                    c = slice(j * P, (j + 1) * P)
                    dve.tensor_tensor(ptl[:, 0:4, c], ps[:, 4, :].rearrange("p (c n) -> p c n", c=4),
                                      pth[:, 0:4, c].bitcast(FP32), ALU.subtract)
                    dve.tensor_tensor(ptl[0:last_rows, 4, c], ps[0:last_rows, 5, 0:P],
                                      pth[0:last_rows, 4, c].bitcast(FP32), ALU.subtract).then_inc(s_ptl, 1)
                    if j == TPB - 1:
                        dve.wait_ge(s_oh, blk + 1)
                        dve.tensor_tensor(ol[:], ps[:, 6:8, :], oh[:].bitcast(FP32), ALU.subtract)\
                            .then_inc(s_ol, 1)
                        for h in range(2):
                            tt = blk * TPB + 2 * h
                            dve.wait_ge(s_y, 2 * blk + h + 1)
                            xs = m.x[:, tt:tt + 2, :]
                            dve.tensor_tensor(xs, xs, ps[:, 6 + h, :].rearrange("p (t n) -> p t n", t=2),
                                              ALU.add).then_inc(s_x, 1)

            @block.tensor
            def _(pe):
                norm_pe(pe, m, ns)
                for n in range(NB * KD):
                    blk, g = n // KD, n % KD
                    pe.wait_ge(ns.lo, ns.blocks + blk + 1)
                    if n >= 4:
                        pe.wait_ge(s_ql, n - 3)
                    k3 = 0
                    for k in range(KD):
                        for st, mo in split_passes((wqh, wql), (m.uh, m.ul)):
                            i = pe.matmul(ps[:, 4 + n % 4, :], st[:, k, g * P:(g + 1) * P],
                                          mo[:, k, blk * BLK:(blk + 1) * BLK], start=k3 == 0, stop=k3 == 5)
                            k3 += 1
                    i.then_inc(s_q, 1)

                def scores(t):
                    b = t // (NT // B)
                    if t == 0:
                        pe.wait_ge(s_ql, NB * KD)
                    if t >= 2:
                        pe.wait_ge(s_sd, t - 1)
                    for g in range(KD):
                        for n, (st, mo) in enumerate(split_passes((qh, ql), (kbh, kbl))):
                            i = pe.matmul(ps[:, 2 * (t % 2) + g, 0:G0 * SC], st[:, g, t * P:(t + 1) * P],
                                          mo[:, b, g].rearrange("p h s -> p (h s)"), start=n == 0, stop=n == 2)
                    i.then_inc(s_s, 1)

                scores(0)
                for blk, j, t in tiles():
                    b = t // (NT // B)
                    if t + 1 < NT:
                        scores(t + 1)
                    pe.wait_ge(s_pn, t + 1)
                    if t:
                        pe.wait_ge(s_ptl, t)
                    for c in range(NC0):
                        n = min(P, KC0 - c * P)
                        i = pe.transpose(ps[0:n, 4 + c // 4, (c % 4) * P:(c % 4 + 1) * P],
                                         pn[:, t % 2, c * P:c * P + n], m.ident[:, :])
                    i.then_inc(s_pt, 1)
                    if j == TPB - 1:
                        pe.wait_ge(s_ptl, t + 1)
                        if blk:
                            pe.wait_ge(s_x, 2 * blk)
                        for g, (c0, c1) in enumerate(halves):
                            for c in range(c0, c1):
                                r = min(P, KC0 - c * P)
                                for n, (st, mo) in enumerate(split_passes((vbh, vbl), (pth, ptl))):
                                    i = pe.matmul(ps[:, 6 + g, :], st[0:r, b, c, g * P:(g + 1) * P],
                                                  mo[0:r, c, :], start=c == c0 and n == 0,
                                                  stop=c == c1 - 1 and n == 2)
                        i.then_inc(s_o, 1)
                        pe.wait_ge(s_ol, blk + 1)
                        for jj in range(TPB):
                            n = 0
                            for g in range(KD):
                                for st, mo in split_passes((oh, ol), (woh, wol)):
                                    i = pe.matmul(ps[:, 6 + jj // 2, (jj % 2) * D:(jj % 2 + 1) * D],
                                                  st[:, g, jj * P:(jj + 1) * P], mo[:, g, :],
                                                  start=n == 0, stop=n == 5)
                                    n += 1
                            if jj % 2:
                                i.then_inc(s_y, 1)



class Step:

    def __init__(self, n, group, chunk, blk, block, ends, mixed=False):
        self.n = n
        self.group = group
        self.chunk, self.blk = chunk, blk
        self.block = block
        self.first, self.last = chunk == 0, ends
        self.mixed = mixed


class Base:

    def __init__(self, lay, i):
        self.at_start = isinstance(i, int) and i == 0
        self.pair = i
        self.n = i * len(lay.body)
        self.block = i * 2 * NB
        self.group = i * 2
        self.chunk = i * 2 * lay.chunks


class Layer:
    def __init__(self, gated, chunks, pairs, tail_chunks):
        self.gated = gated
        self.chunks = chunks
        self.width = (4 + 2 if gated else 2 + 2) * P
        self.body = self.steps([chunks, chunks])
        self.tail = self.steps(tail_chunks, mixed=tail_chunks[1] != chunks)
        self.pairs = pairs
        self.hbanks = 2 if gated else 4

    def steps(self, chunks, mixed=False):
        out = []
        for g, nc_ in enumerate(chunks):
            for blk in range(NB):
                for c in range(nc_):
                    out.append(Step(len(out), g, c, blk, g * NB + blk, c == nc_ - 1, mixed and g == 1))
        return out


def walk(lay, eng, lead, early, late):

    def some(steps, base, after, base_after):
        for st in steps:
            ahead = st.n + lead
            if ahead < len(steps):
                early(steps[ahead], base)
            elif after:
                early(after[ahead - len(steps)], base_after)
            late(st, base)

    for st in lay.body[:lead]:
        early(st, Base(lay, 0))
    some(lay.body, Base(lay, 0), lay.body, Base(lay, 1))
    with eng.Fori(1, lay.pairs) as i:
        some(lay.body, Base(lay, i), lay.body, Base(lay, i + 1))
    some(lay.tail, Base(lay, lay.pairs), None, None)


def experts(nc, m, a, tag, lay, raw_in):
    ps = m.ps
    gated, CH, W = lay.gated, lay.chunks, lay.width
    n_in = 2 if gated else 1
    lead_w = P * KD * n_in
    w_dram = a[f"{tag}_w"]
    with ExitStack() as ctx:
        def sb(name, shape, dt=FP32):
            return ctx.enter_context(nc.sbuf_tensor(f"{tag}_{name}", shape, dt))

        def sem(name):
            return ctx.enter_context(nc.semaphore(f"{tag}_{name}"))

        wh, wl = (sb(f"w{n}", [P, 2, CH * W], FP32R) for n in "hl")
        yT = sb("yT", [P, KD, T])
        wT = m.z[0:E + 1, :, :, :].rearrange("p a t d -> p (a t d)")
        bcol = sb("bcol", [P, 2, CH]) if not gated else None
        g_dram = nc.dram_tensor(f"{tag}_gate_rows", [E + 1, T], FP32).ap()
        s_split, s_wh = sem("split"), sem("wh")
        s_gd = sem("gd")

        def split(pool, group, chunk, par):
            c = slice(chunk * W, (chunk + 1) * W)
            pool.tensor_tensor(wh[:, par, c], m.raw[:, c], m.one[:].to_broadcast([P, W]), ALU.mult).then_inc(s_wh, 1)
            pool.wait_ge(s_wh, group * CH + chunk + 1)
            pool.tensor_tensor(wl[:, par, c], m.raw[:, c], wh[:, par, c].bitcast(FP32), ALU.subtract)\
                .then_inc(s_split, 1)

        with ExitStack() as c2:
            def sb2(name, shape, dt=FP32):
                return c2.enter_context(nc.sbuf_tensor(f"{tag}_{name}", shape, dt))

            wg = sb2("wg", [P, KD, E])
            wgh, wgl = (sb2(f"wg{n}", [P, KD, E], FP32R) for n in "hl")
            bias = sb2("bias", [P, E])
            tri = sb2("tri", [P, E, E]) if gated else None
            b2 = sb2("b2", [E, D]) if not gated else None
            lg = sb2("lg", [P, NT, E])
            gt = sb2("gt", [P, NT, E, E])
            eq = sb2("eq", [P, NT, E, E]) if gated else None
            rank = sb2("rank", [P, NT, E])
            mk = sb2("mk", [P, NT, E])
            mx = sb2("mx", [P, NT])
            sh = sb2("sh", [P, NT, E])
            ex = sb2("ex", [P, NT, E])
            em = sb2("em", [P, NT, E])
            sm = sb2("sm", [P, NT])
            rc = sb2("rc", [P, NT])
            w = sb2("w", [P, NT, E + 1])
            ns = m.norm
            s_par, s_wg, s_lt, s_ltc, s_lg, s_sh, s_ex, s_w, s_wt, s_wTs, s_b2, s_y0 = (
                sem(f"r_{n}") for n in ("par", "wg", "lt", "ltc", "lg", "sh", "ex", "w", "wt", "wTs", "b2", "y0"))
            s_ch = sem("r_ch")
            n_par = 3 if gated else 3

            with nc.Block() as block:
                @block.sync
                def _(sp):
                    sp.dma_start(wg[:], a[f"{tag}_wg"]).then_inc(s_par, 16)
                    sp.dma_start(bias[:], a[f"{tag}_bias"].partition_broadcast(P)).then_inc(s_par, 16)
                    if gated:
                        sp.dma_start(tri[:], a["c_tri"].partition_broadcast(P)).then_inc(s_par, 16)
                    else:
                        sp.dma_start(b2[:], a[f"{tag}_b2"]).then_inc(s_par, 16)
                    sp.wait_ge(s_par, 16 * n_par)

                @block.gpsimd
                def _(pool):
                    norm_pool(pool, m, ns, twice=False)
                    pool.memset(w[:], 1.0).then_inc(s_wg, 1)
                    pool.wait_ge(s_wg, 2)
                    pool.tensor_tensor(wgl[:], wg[:], wgh[:].bitcast(FP32), ALU.subtract).then_inc(s_wg, 1)
                    if gated:
                        pool.memset(yT[:], 0.0)
                    pool.wait_ge(raw_in, 16)
                    if not gated:
                        pool.tensor_tensor(bcol[:, 0], m.raw[:, CH * W:CH * W + CH],
                                           m.one[:].to_broadcast([P, CH]), ALU.mult)
                    for c in range(CH):
                        split(pool, 0, c, 0)

                @block.scalar
                def _(act):
                    act.wait_ge(s_par, 16 * n_par)
                    act.activation(wgh[:], wg[:], ACT.Copy).then_inc(s_wg, 1)
                    norm_act(act, m, ns)
                    for blk in range(NB):
                        act.wait_ge(s_lt, blk + 1)
                        act.activation(wT[0:E, blk * BLK:(blk + 1) * BLK], ps[0:E, 4 + blk, :], ACT.Copy)\
                            .then_inc(s_ltc, 1)
                    act.wait_ge(s_sh, 1)
                    act.activation(ex[:], sh[:], ACT.Exp).then_inc(s_ex, 1)
                    for blk in range(NB):
                        act.wait_ge(s_wt, blk + 1)
                        act.activation(wT[:, blk * BLK:(blk + 1) * BLK], ps[0:E + 1, blk, :], ACT.Copy)\
                            .then_inc(s_wTs, 1)
                    if not gated:
                        for blk in range(NB):
                            for k in range(KD):
                                n = blk * KD + k
                                act.wait_ge(s_b2, n + 1)
                                act.activation(yT[:, k, blk * BLK:(blk + 1) * BLK], ps[:, 4 + n % 4, :],
                                               ACT.Copy).then_inc(s_y0, 1)

                @block.vector
                def _(dve):
                    norm_dve(dve, m, ns)
                    dve.wait_ge(s_wg, 1)
                    dve.wait_ge(s_par, 16 * n_par)
                    ch = Chain(dve, s_ch)

                    def then(instruction):
                        ch.mark(instruction)
                        ch.wait()

                    def over_j(v):
                        return v.unsqueeze(2).to_broadcast([P, NT, E, E])

                    def over_e(v):
                        return v.unsqueeze(3).to_broadcast([P, NT, E, E])

                    dve.wait_ge(s_lg, 1)
                    then(dve.tensor_tensor(lg[:], ps[:, 4, 0:NT * E].rearrange("p (t e) -> p t e", e=E),
                                           bias[:].unsqueeze(1).to_broadcast([P, NT, E]), ALU.add))
                    dve.reduce_max(mx[:], lg[:], AX.X).then_inc(s_ch, 1)
                    ch.n += 1
                    then(dve.tensor_tensor(gt[:], over_j(lg[:]), over_e(lg[:]), ALU.is_gt))
                    dve.tensor_tensor(sh[:], lg[:], mx[:].unsqueeze(2).to_broadcast([P, NT, E]),
                                      ALU.subtract).then_inc(s_sh, 1)
                    if gated:
                        then(dve.tensor_tensor(eq[:], over_j(lg[:]), over_e(lg[:]), ALU.is_equal))
                        then(dve.tensor_tensor(eq[:], eq[:], tri[:].unsqueeze(1).to_broadcast([P, NT, E, E]),
                                               ALU.mult))
                        then(dve.tensor_tensor(gt[:], gt[:], eq[:], ALU.add))
                    then(dve.reduce_sum(rank[:], gt[:], AX.X))
                    then(dve.tensor_scalar(mk[:], rank[:], float(TOPK0 if gated else TOPK1), None, ALU.is_lt))
                    dve.wait_ge(s_ex, 1)
                    then(dve.tensor_tensor(em[:], ex[:], mk[:], ALU.mult))
                    then(dve.reduce_sum(sm[:], em[:], AX.X))
                    then(dve.reciprocal(rc[:], sm[:]))
                    dve.tensor_tensor(w[:, :, 0:E], em[:], rc[:].unsqueeze(2).to_broadcast([P, NT, E]),
                                      ALU.mult).then_inc(s_w, 1)

                @block.tensor
                def _(pe):
                    norm_pe(pe, m, ns)
                    pe.wait_ge(s_wg, 3)
                    for blk in range(NB):
                        pe.wait_ge(ns.lo, ns.blocks + blk + 1)
                        n = 0
                        for k in range(KD):
                            for st, mo in split_passes((wgh, wgl), (m.uh, m.ul)):
                                i = pe.matmul(ps[0:E, 4 + blk, :], st[:, k, :],
                                              mo[:, k, blk * BLK:(blk + 1) * BLK], start=n == 0, stop=n == 5)
                                n += 1
                        i.then_inc(s_lt, 1)
                    for t in range(NT):
                        if t % TPB == 0:
                            pe.wait_ge(s_ltc, t // TPB + 1)
                        i = pe.transpose(ps[:, 4, t * E:(t + 1) * E], wT[0:E, t * P:(t + 1) * P],
                                         m.ident[0:E, 0:E])
                    i.then_inc(s_lg, 1)
                    pe.wait_ge(s_w, 1)
                    for t in range(NT):
                        i = pe.transpose(ps[0:E + 1, t // TPB, (t % TPB) * P:(t % TPB + 1) * P],
                                         w[:, t, :], m.ident[:, :])
                        if t % TPB == TPB - 1:
                            i.then_inc(s_wt, 1)
                    if not gated:
                        for blk in range(NB):
                            pe.wait_ge(s_wTs, blk + 1)
                            for k in range(KD):
                                n = blk * KD + k
                                if n >= 4:
                                    pe.wait_ge(s_y0, n - 3)
                                pe.matmul(ps[:, 4 + n % 4, :], b2[:, k * P:(k + 1) * P],
                                          wT[0:E, blk * BLK:(blk + 1) * BLK], start=True, stop=True)\
                                    .then_inc(s_b2, 1)

        with ExitStack() as c3:
            def sb3(name, shape, dt=FP32):
                return c3.enter_context(nc.sbuf_tensor(f"{tag}_{name}", shape, dt))

            gates = sb3("gates", [P, 3 if gated else 2, T])
            sa = sb3("sa", [P, 2, BLK])
            tt = sb3("tt", [P, 2, BLK]) if gated else None
            g = sb3("g", [P, 2, BLK])
            hh, hl = (sb3(f"h{n}", [P, 4, BLK], FP32R) for n in "hl")
            s_g = [sem(f"g{n}") for n in range(2)]
            s_gmix = [sem(f"gmix{n}") for n in range(NMIX0)] if gated else None
            s_h, s_sa, s_t, s_gate, s_hh, s_hl, s_out, s_y = (
                sem(n) for n in ("h", "sa", "t", "gate", "hh", "hl", "out", "y"))
            s_yt, s_x = sem("yt"), sem("x")
            last_pair = lay.pairs
            HB = lay.hbanks

            def gate_of(st):
                return 2 - st.chunk if st.mixed else st.group

            with nc.Block() as block:
                @block.sync
                def _(sp):
                    def weights(group, splits_before):
                        sp.wait_ge(s_split, splits_before)
                        if isinstance(group, int) and gated and group == E + 1:
                            sp.dma_start(m.raw[:, 0:NMIX0 * W], a["f0_wmix"]).then_inc(raw_in, 16)
                        else:
                            sp.dma_start(m.raw[:, 0:w_dram.shape[2]], w_dram[group]).then_inc(raw_in, 16)

                    def gate_row(group, par, steps_before):
                        if steps_before is not None:
                            sp.wait_ge(s_gate, steps_before)
                        sp.dma_start(gates[:, par, :], g_dram[group].partition_broadcast(P))\
                            .then_inc(s_g[par], 16)

                    n2 = len(lay.body)
                    sp.wait_ge(s_wTs, NB)
                    sp.dma_start(g_dram, wT).then_inc(s_gd, 16)
                    sp.wait_ge(s_gd, 16)
                    gate_row(0, 0, None)
                    weights(1, CH)
                    gate_row(1, 1, None)

                    def pair(i):
                        weights(2 * i, 2 * i * CH)
                        gate_row(2 * i, 0, i * n2 - n2 // 2)
                        weights(2 * i + 1, (2 * i + 1) * CH)
                        gate_row(2 * i + 1, 1, i * n2)

                    with sp.Fori(1, last_pair) as i:
                        pair(i)
                    if not gated:
                        pair(last_pair)
                    else:
                        i = last_pair
                        weights(2 * i, 2 * i * CH)
                        gate_row(2 * i, 0, i * n2 - n2 // 2)
                        weights(2 * i + 1, (2 * i + 1) * CH)
                        for mix in range(NMIX0):
                            par = 2 - mix
                            if mix:
                                sp.wait_ge(s_gate, i * n2 + (mix - 1) * (n2 // 2))
                            for e in range(MIX0):
                                sp.dma_start(gates[e * REM0:(e + 1) * REM0, par, :],
                                             g_dram[mix * MIX0 + e].partition_broadcast(REM0))\
                                    .then_inc(s_gmix[mix], 16)
                            sp.dma_start(gates[MIX0 * REM0:P, par, :],
                                         g_dram[E].partition_broadcast(P - MIX0 * REM0))\
                                .then_inc(s_gmix[mix], 16)

                @block.gpsimd
                def _(pool):
                    def group_split(group, par, chunks, steps_before):
                        pool.wait_ge(raw_in, 16 * group + 16)
                        if steps_before is not None:
                            pool.wait_ge(s_out, steps_before)
                        if not gated:
                            pool.tensor_tensor(bcol[:, par], m.raw[:, CH * W:CH * W + CH],
                                           m.one[:].to_broadcast([P, CH]), ALU.mult)
                        for c in range(chunks):
                            split(pool, group, c, par)

                    half = len(lay.body) // 2
                    group_split(1, 1, CH, None)
                    with pool.Fori(1, last_pair) as i:
                        group_split(2 * i, 0, CH, i * 2 * half - half)
                        group_split(2 * i + 1, 1, CH, i * 2 * half)
                    i = last_pair
                    group_split(2 * i, 0, CH, i * 2 * half - half)
                    group_split(2 * i + 1, 1, NMIX0 if gated else CH, i * 2 * half)

                @block.scalar
                def _(act):
                    def early(st, base):
                        n = base.n + st.n
                        act.wait_ge(s_h, n + 1)
                        if not (base.at_start and st.n < 2):
                            act.wait_ge(s_gate, n - 1)
                        if gated:
                            act.activation(sa[:, st.n % 2], ps[:, 2 * (st.n % 2), :], ACT.Silu)\
                                .then_inc(s_sa, 1)
                        else:
                            if st.blk == 0 and st.chunk == 0:
                                act.wait_ge(s_split, base.chunk + st.group * CH + 1)
                            act.activation(sa[:, st.n % 2], ps[:, st.n % 4, :], ACT.Gelu,
                                           bias=bcol[:, st.group, st.chunk:st.chunk + 1]).then_inc(s_sa, 1)

                    def late(st, base):
                        n = base.n + st.n
                        act.wait_ge(s_gate, n + 1)
                        if not (base.at_start and st.n < 4):
                            act.wait_ge(s_out, n - 3)
                        act.activation(hh[:, st.n % 4], g[:, st.n % 2], ACT.Copy).then_inc(s_hh, 1)

                    walk(lay, act, 1, early, late)

                @block.vector
                def _(dve):
                    def add_out(block, par_block, blk, steps):
                        dve.wait_ge(s_out, steps)
                        bank = 4 + 2 * (par_block % 2)
                        y = yT[:, :, blk * BLK:(blk + 1) * BLK]
                        dve.tensor_tensor(y, y, ps[:, bank:bank + 2, :], ALU.add).then_inc(s_y, 1)

                    def early(st, base):
                        n = base.n + st.n
                        dve.wait_ge(s_sa, n + 1)
                        if st.mixed:
                            if st.blk == 0:
                                dve.wait_ge(s_gmix[st.chunk], 16 * (MIX0 + 1))
                        elif st.blk == 0 and st.chunk == 0:
                            dve.wait_ge(s_g[st.group], base.pair * 16 + 16)
                        src = sa[:, st.n % 2]
                        if gated:
                            dve.tensor_tensor(tt[:, st.n % 2], src, ps[:, 2 * (st.n % 2) + 1, :], ALU.mult)\
                                .then_inc(s_t, 1)
                            dve.wait_ge(s_t, n + 1)
                            src = tt[:, st.n % 2]
                        elif not (base.at_start and st.n < 2):
                            dve.wait_ge(s_hl, n - 1)
                        dve.tensor_tensor(g[:, st.n % 2], src,
                                          gates[:, gate_of(st), st.blk * BLK:(st.blk + 1) * BLK],
                                          ALU.mult).then_inc(s_gate, 1)

                    def late(st, base):
                        n = base.n + st.n
                        dve.wait_ge(s_hh, n + 1)
                        dve.tensor_tensor(hl[:, st.n % 4], g[:, st.n % 2], hh[:, st.n % 4].bitcast(FP32),
                                          ALU.subtract).then_inc(s_hl, 1)
                        if st.chunk == 2 and not (base.at_start and st.block == 0):
                            add_out(base.block + st.block, st.block - 1, (st.blk - 1) % NB,
                                    base.n + st.n - st.chunk)

                    walk(lay, dve, 1, early, late)
                    total = last_pair * len(lay.body) + len(lay.tail)
                    add_out(None, 1, NB - 1, total)
                    for t in range(0, NT, 2):
                        dve.wait_ge(s_yt, t // 2 + 1)
                        xs = m.x[:, t:t + 2, :]
                        dve.tensor_tensor(xs, xs, ps[:, t // 2, :].rearrange("p (t n) -> p t n", t=2),
                                          ALU.add).then_inc(s_x, 1)

                @block.tensor
                def _(pe):
                    def early(st, base):
                        n = base.n + st.n
                        if st.blk == 0:
                            pe.wait_ge(s_split, base.chunk + st.group * CH + st.chunk + 1)
                        if not (base.at_start and st.n < HB):
                            if gated:
                                pe.wait_ge(s_gate, n - 1)
                            else:
                                pe.wait_ge(s_sa, n - 3)
                        for w in range(n_in):
                            bank = 2 * (st.n % 2) + w if gated else st.n % 4
                            q = 0
                            for k in range(KD):
                                col = st.chunk * W + (w * KD + k) * P
                                for sta, mo in split_passes((wh, wl), (m.uh, m.ul)):
                                    i = pe.matmul(ps[:, bank, :], sta[:, st.group, col:col + P],
                                                  mo[:, k, st.blk * BLK:(st.blk + 1) * BLK],
                                                  start=q == 0, stop=q == 5)
                                    q += 1
                        i.then_inc(s_h, 1)

                    def late(st, base):
                        n = base.n + st.n
                        pe.wait_ge(s_hl, n + 1)
                        if st.first and not (base.at_start and st.block < 2):
                            pe.wait_ge(s_y, base.block + st.block - 1)
                        for k in range(KD):
                            bank = 4 + 2 * (st.block % 2) + k
                            col = st.chunk * W + lead_w + k * P
                            for q, (sta, mo) in enumerate(split_passes((wh, wl), (hh, hl))):
                                i = pe.matmul(ps[:, bank, :], sta[:, st.group, col:col + P],
                                              mo[:, st.n % 4, :], start=st.first and q == 0,
                                              stop=st.last and q == 2)
                        i.then_inc(s_out, 1)

                    walk(lay, pe, 2 if gated else 3, early, late)
                    pe.wait_ge(s_y, last_pair * 2 * NB + 2 * NB)
                    for t in range(NT):
                        for k in range(KD):
                            i = pe.transpose(ps[:, t // 2, (t % 2) * D + k * P:(t % 2) * D + (k + 1) * P],
                                             yT[:, k, t * P:(t + 1) * P], m.ident[:, :])
                        if t % 2:
                            i.then_inc(s_yt, 1)



HEADS1 = [(b, h) for b in range(B) for h in range(H1)]
TQ = S // P
NTQ = len(HEADS1) * TQ
NSTK = 2 * (TQ // 4) + 3


class Bank:

    def __init__(self, kind, *at):
        self.kind, self.at = kind, at


class BankOrder:

    def __init__(self):
        self.uses = [Bank("stack", 0, n) for n in range(NSTK)] + [Bank("scores", 0, n) for n in range(2)]
        self.first = len(self.uses)
        self.step = []
        for g in range(NTQ + 2):
            head, t = divmod(g, TQ)
            now = []
            if g < NTQ:
                now.append(Bank("context", g))
            if g % 2 == 0 and 2 <= g:
                now.append(Bank("values", (g - 2) // 2))
            if g % 2 == 1 and 3 <= g:
                now.append(Bank("project", (g - 3) // 2))
            if g < NTQ:
                stacks = {6: (0,), 7: (1,), 0: (6,), 1: (2,), 2: (3,), 3: (4,), 4: (5,)}.get(t, ())
                ahead = head + (2 if t >= 6 else 1)
                if g == 0:
                    stacks = (0, 1, 6)
                if ahead < len(HEADS1):
                    now += [Bank("stack", ahead, n) for n in stacks]
                if t == 5 and ahead < len(HEADS1):
                    now += [Bank("scores", ahead, n) for n in range(2)]
            self.step.append(now)
            self.uses += now
        acts = dves = 0
        self.find = {}
        for k, u in enumerate(self.uses):
            u.k = k
            u.bank = 6 + k % 2
            if u.kind in ("stack", "scores"):
                acts += 1
            else:
                dves += 1
            u.act, u.dve = acts, dves
            self.find[(u.kind, *u.at)] = u

    def stacked(self, head):
        return max(self.find[("stack", head, n)].act for n in range(NSTK))

    def transposed(self, head, stacks):
        return max(self.find[("stack", head, n)].k for n in stacks) + 1

    def wait_free(self, pe, u, s_act, s_dve):
        if u.k >= 2:
            old = self.uses[u.k - 2]
            if old.kind in ("stack", "scores"):
                pe.wait_ge(s_act, old.act)
            else:
                pe.wait_ge(s_dve, old.dve)


def attention1(nc, m, a, raw_in):
    ps = m.ps
    with ExitStack() as ctx:
        def sb(name, shape, dt=FP32):
            return ctx.enter_context(nc.sbuf_tensor(f"b_{name}", shape, dt))

        def sem(name):
            return ctx.enter_context(nc.semaphore(f"b_{name}"))

        NH = len(HEADS1)
        qs = sb("qs", [P, NH, TQ, DH1])
        kvs = sb("kvs", [P, NH, NKT, 2 * DH1])
        woh, wol = (sb(f"wo{n}", [P, H1, D], FP32R) for n in "hl")
        maskm = sb("maskm", [P, B, SCP], FP32R)
        row0 = sb("row0", [P, P], FP32R)
        RAWS = 3
        raw = sb("raw", [P, RAWS, TQ, P])
        bo = raw[:, 2, 0:2, :].rearrange("p k n -> p (k n)")

        with ExitStack() as c2:
            def sb2(name, shape, dt=FP32):
                return c2.enter_context(nc.sbuf_tensor(f"b_{name}", shape, dt))

            wraw = m.raw[:, 0:KD * 3 * D].rearrange("p (k n) -> p k n", k=KD)
            oraw = m.raw[:, KD * 3 * D:KD * 3 * D + H1 * D].rearrange("p (h n) -> p h n", h=H1)
            craw = m.raw[0:HC, 2560:2560 + 4 * D].rearrange("p (k n) -> p k n", k=2)
            wh, wl = (sb2(f"w{n}", [P, KD, 3 * D], FP32R) for n in "hl")
            wch, wcl = (sb2(f"wc{n}", [HC, 2, 2 * D], FP32R) for n in "hl")
            ll_gb = sb2("ll_gb", [P, 2, KD])
            gq, gk = sb2("gq", [P, DH1]), sb2("gk", [P, DH1])
            zf = sb2("zf", [P, KD, BLK])
            sq = sb2("sq", [P, 2, 2 * H1, DH1])
            ss = sb2("ss", [P, 2, 2 * H1])
            r1 = sb2("r1", [P, 2, 2 * H1])
            rr = sb2("rr", [P, 2, 2 * H1])
            half = sb2("half", [P, 2 * H1])
            qk = sb2("qk", [P, 2, 2 * H1, DH1])
            mku = sb2("mku", [1, B, SC], UINT8)
            mkf = sb2("mkf", [1, B, SC])
            ns = m.norm
            s_w, s_par, s_wh, s_wl, s_mk = (sem(n) for n in ("w", "par", "wh", "wl", "mk"))
            s_gq, s_p, s_sq, s_v, s_ss, s_r1, s_r, s_qk, s_g = (
                sem(n) for n in ("gq", "p", "sq", "v", "ss", "r1", "r", "qk", "g"))

            qkr = raw[:, 0:2, :, :].rearrange("p a k n -> p (a k n)").rearrange("p (s n) -> p s n", s=4)
            units = [(t, t // TQ, t % TQ) for t in range(NT)] + [(NT + b, b, TQ) for b in range(B)]

            def shape_of(u):
                return (P, 2 * H1) if u < NT else (SCP, H1)

            with nc.Block() as block:
                @block.sync
                def _(sp):
                    sp.dma_start(ll_gb[:], a["ll_gb"]).then_inc(s_par, 16)
                    sp.dma_start(gq[:], a["qn_g"].partition_broadcast(P)).then_inc(s_par, 16)
                    sp.dma_start(gk[:], a["kn_g"].partition_broadcast(P)).then_inc(s_par, 16)
                    sp.dma_start(bo, a["bo"].partition_broadcast(P)).then_inc(s_par, 16)
                    sp.dma_start(mku[:], a["mask"].rearrange("(o b) s -> o b s", o=1)).then_inc(s_par, 16)
                    sp.dma_start(wraw, a["wqkv1"]).then_inc(s_w, 16)
                    sp.dma_start(craw, a["wc1"]).then_inc(s_w, 16)
                    for n in range(2):
                        sp.dma_start(oraw[n * DH1:(n + 1) * DH1], a["wo1"]).then_inc(s_w, 16)
                    sp.wait_ge(s_par, 80)

                @block.gpsimd
                def _(pool):
                    pool.memset(half[:], -0.5).then_inc(s_mk, 1)
                    pool.memset(maskm[:].bitcast(FP32), 0.0).then_inc(s_mk, 1)
                    pool.memset(row0[:].bitcast(FP32), 0.0).then_inc(s_mk, 1)
                    norm_pool(pool, m, ns, twice=True)
                    pool.wait_ge(s_wh, 2)
                    pool.tensor_tensor(wl[:], wraw, wh[:].bitcast(FP32), ALU.subtract).then_inc(s_wl, 1)
                    pool.tensor_tensor(wcl[:], craw, wch[:].bitcast(FP32), ALU.subtract).then_inc(s_wl, 1)
                    pool.wait_ge(s_wh, 3)
                    pool.tensor_tensor(wol[:], oraw, woh[:].bitcast(FP32), ALU.subtract).then_inc(s_wl, 1)

                    def rms(n):
                        u = units[n][0]
                        rows, w = shape_of(u)
                        sl = n % 2
                        pool.wait_ge(s_ss, n + 1)
                        pool.tensor_scalar(r1[0:rows, sl, 0:w], ss[0:rows, sl, 0:w], 1.0 / DH1, 1e-16,
                                           ALU.mult, ALU.max).then_inc(s_r1, 1)
                        pool.wait_ge(s_r1, n + 1)
                        pool.tensor_tensor(rr[0:rows, sl, 0:w], r1[0:rows, sl, 0:w], half[0:rows, 0:w],
                                           ALU.pow).then_inc(s_r, 1)

                    for n in range(len(units)):
                        rms(n)

                @block.scalar
                def _(act):
                    act.wait_ge(s_w, 64)
                    act.activation(wh[:], wraw, ACT.Copy).then_inc(s_wh, 1)
                    act.activation(wch[:], craw, ACT.Copy).then_inc(s_wh, 1)
                    act.activation(woh[:], oraw, ACT.Copy).then_inc(s_wh, 1)
                    norm_act(act, m, ns, zf)
                    for n, (u, b, t) in enumerate(units):
                        rows, w = shape_of(u)
                        bank = 4 + 2 * (n % 2)
                        act.wait_ge(s_p, n + 1)
                        if n >= 2:
                            act.wait_ge(s_ss, n - 1)
                        act.activation(sq[0:rows, n % 2, 0:w].rearrange("p h d -> p (h d)"),
                                       ps[0:rows, bank, 0:w * DH1], ACT.Square).then_inc(s_sq, 1)
                        act.activation(kvs[0:rows, b * H1:(b + 1) * H1, t, DH1:2 * DH1],
                                       ps[0:rows, bank + 1, 0:D].rearrange("p (h d) -> p h d", h=H1),
                                       ACT.Copy)
                        if n >= 4:
                            act.wait_ge(s_qk, n - 3)
                        act.activation(qkr[0:rows, n % 4, 0:w * DH1], ps[0:rows, bank, 0:w * DH1],
                                       ACT.Copy).then_inc(s_v, 1)

                @block.vector
                def _(dve):
                    dve.wait_ge(s_par, 80)
                    dve.tensor_scalar(gq[:], gq[:], float(DH1) ** -0.5, None, ALU.mult).then_inc(s_gq, 1)
                    dve.tensor_copy(mkf[:], mku[:]).then_inc(s_mk, 1)
                    norm_dve(dve, m, ns, ll_gb, zf)
                    dve.wait_ge(s_mk, 4)
                    dve.memset(maskm[0:1, :, SC:SCP].bitcast(FP32), NEG)
                    dve.memset(row0[0:1, :].bitcast(FP32), 1.0)
                    dve.tensor_scalar(maskm[0:1, :, 0:SC], mkf[:], 1.0, -NEG, ALU.subtract, ALU.mult)

                    def squares(n):
                        rows, w = shape_of(units[n][0])
                        dve.wait_ge(s_sq, n + 1)
                        if n >= 2:
                            dve.wait_ge(s_r1, n - 1)
                        dve.reduce_sum(ss[0:rows, n % 2, 0:w], sq[0:rows, n % 2, 0:w], AX.X).then_inc(s_ss, 1)

                    def normed(n):
                        rows, w = shape_of(units[n][0])
                        dve.wait_ge(s_r, n + 1)
                        dve.wait_ge(s_v, n + 1)
                        if n >= 2:
                            dve.wait_ge(s_g, n - 1)
                        dve.tensor_tensor(qk[0:rows, n % 2, 0:w],
                                          qkr[0:rows, n % 4, 0:w * DH1]
                                          .rearrange("p (h d) -> p h d", h=w),
                                          rr[0:rows, n % 2, 0:w].unsqueeze(2).to_broadcast([rows, w, DH1]),
                                          ALU.mult).then_inc(s_qk, 1)

                    def gains(n):
                        u, b, t = units[n]
                        rows, w = shape_of(u)
                        hs = slice(b * H1, (b + 1) * H1)
                        dve.wait_ge(s_qk, n + 1)
                        if u < NT:
                            dve.tensor_tensor(qs[:, hs, t, :], qk[:, n % 2, 0:H1],
                                              gq[:].unsqueeze(1).to_broadcast([P, H1, DH1]), ALU.mult)
                        dve.tensor_tensor(kvs[0:rows, hs, t, 0:DH1], qk[0:rows, n % 2, w - H1:w],
                                          gk[0:rows].unsqueeze(1).to_broadcast([rows, H1, DH1]),
                                          ALU.mult).then_inc(s_g, 1)

                    dve.wait_ge(s_gq, 1)
                    for n in range(len(units) + 2):
                        if n < len(units):
                            squares(n)
                        if 1 <= n <= len(units):
                            normed(n - 1)
                        if n >= 2:
                            gains(n - 2)

                @block.tensor
                def _(pe):
                    norm_pe(pe, m, ns)
                    pe.wait_ge(s_wl, 2)
                    for n, (u, b, t) in enumerate(units):
                        rows, w = shape_of(u)
                        bank = 4 + 2 * (n % 2)
                        if u < NT:
                            pe.wait_ge(ns.lo, ns.blocks + u // TPB + 1)
                        if n >= 2:
                            pe.wait_ge(s_v, n - 1)
                        parts_ = ((0, 0, 2 * H1 * DH1), (1, 2 * D, D)) if u < NT else ((0, 0, D), (1, D, D))
                        for bk, col, width in parts_:
                            q = 0
                            for k in range(2):
                                if u < NT:
                                    pairs = split_passes((m.uh, m.ul), (wh, wl))
                                else:
                                    pairs = split_passes((m.cxh, m.cxl), (wch, wcl))
                                for st, mo in pairs:
                                    sta = st[:, k, u * P:(u + 1) * P] if u < NT else st[:, k, b, :]
                                    i = pe.matmul(ps[0:rows, bank + bk, 0:width], sta,
                                                  mo[:, k, col:col + width], start=q == 0, stop=q == 5)
                                    q += 1
                        i.then_inc(s_p, 1)

        order = BankOrder()
        qst = sb("qst", [P, 2, 2, S], FP32R)
        kst = sb("kst", [P, 2, NK1], FP32R)
        vst = sb("vst", [P, 2, NKT, 2 * DH1], FP32R)
        qc = m.z[:, :, :, :].rearrange("p a t d -> p (a t d)").rearrange("p (t w e d) -> p t w e d", t=TQ, w=2, e=2)
        kc = sb("kc", [P, NKT, 2, DH1])
        pth, ptl = (u[:, :, :].rearrange("p k t -> p (k t)").rearrange("p (c n) -> p c n", c=TQ)
                    for u in (m.uh, m.ul))
        pch, pcl = (sb(f"pc{n}", [SCP, BLK], FP32R) for n in "hl")
        sctx = sb("sctx", [P, 2, TQ, SCP])
        nmc = sb("nmc", [P, 2, TQ])
        nml, nmx, sml, smc = (sb(n, [P, NTQ]) for n in ("nml", "nmx", "sml", "smc"))
        sm = rc = sml
        ex = sb("ex", [P, 2, NK1])
        oh, ol = (sb(f"o{n}", [P, 2 * P], FP32R) for n in "hl")
        s_bo, s_hi2, s_cat, s_vst = (sem(n) for n in ("bo", "cath", "cat", "vst"))
        s_s, s_nmc, s_nml, s_mx, s_e, s_sm, s_rc, s_t, s_raw, s_r, s_phi, s_plo, s_dlo, s_pc, s_oh, s_act, s_dve = (
            sem(n) for n in ("s", "nmc", "nml", "mx", "e", "sm", "rc", "t", "raw", "bank", "phi", "plo", "dlo",
                             "pc", "oh", "act", "dve"))
        DVE_TILES, POOL_TILES = slice(0, 3), slice(3, TQ)

        KEY_ROWS = ((P, slice(0, TQ)), (SCP, slice(TQ, NKT)))

        def slot(g):
            return ps[:, 2 * (g % 2):2 * (g % 2) + 2, :].rearrange("p k n -> p (k n)")

        def columns(g):
            return slice((g % 4) * P, (g % 4 + 1) * P)

        HALVES = (slice(0, 4), slice(4, TQ))

        def twice(v):
            return v.unsqueeze(2).to_broadcast([P, 4, 2, DH1])

        def columns_free(eng, g):
            if g >= 4:
                eng.wait_ge(s_r, order.find[("values", g // 2 - 2)].k + 1)

        with nc.Block() as block:
            @block.sync
            def _(sp):
                sp.dma_start(m.raw[:, :], a["f1_w"][0]).then_inc(raw_in, 16)

            @block.gpsimd
            def _(pool):
                def lower_queries(head, n):
                    pool.wait_ge(s_hi2, 4 * head + n + 1)
                    ts = HALVES[n]
                    pool.tensor_tensor(qc[:, ts, 1].bitcast(FP32R), twice(qs[:, head, ts]), qc[:, ts, 0],
                                       ALU.subtract).then_inc(s_cat, 1)

                def lower_keys(head):
                    pool.wait_ge(s_hi2, 4 * head + 3)
                    for rows, ts in KEY_ROWS:
                        i = pool.tensor_tensor(kc[0:rows, ts, 1].bitcast(FP32R), kvs[0:rows, head, ts, 0:DH1],
                                               kc[0:rows, ts, 0], ALU.subtract)
                    i.then_inc(s_cat, 1)

                def lower_values(head):
                    pool.wait_ge(s_hi2, 4 * head + 4)
                    vb = vst[:, head % 2]
                    for rows, ts in KEY_ROWS:
                        i = pool.tensor_tensor(vb[0:rows, ts, DH1:2 * DH1], kvs[0:rows, head, ts, DH1:2 * DH1],
                                               vb[0:rows, ts, 0:DH1].bitcast(FP32), ALU.subtract)
                    i.then_inc(s_vst, 1)

                lower_queries(0, 0)
                lower_queries(0, 1)
                lower_keys(0)
                lower_values(0)
                lower_queries(1, 0)
                lower_queries(1, 1)
                lower_keys(1)
                for g in range(NTQ):
                    pool.wait_ge(s_phi, g + 1)
                    pool.tensor_tensor(ptl[:, POOL_TILES, columns(g)], raw[:, g % RAWS, POOL_TILES],
                                       pth[:, POOL_TILES, columns(g)].bitcast(FP32), ALU.subtract)\
                        .then_inc(s_plo, 1)
                    head, t = divmod(g, TQ)
                    if t == 2 and head + 1 < NH:
                        lower_values(head + 1)
                    if t in (4, 5) and head + 2 < NH:
                        lower_queries(head + 2, t - 4)
                    if t == 6 and head + 2 < NH:
                        lower_keys(head + 2)

            @block.scalar
            def _(act):
                def exps(g):
                    head, t = divmod(g, TQ)
                    act.wait_ge(s_mx, g + 1)
                    if t == 0:
                        act.wait_ge(s_act, order.find[("scores", head, 1)].act)
                    if g >= 2:
                        act.wait_ge(s_t, g - 1)
                        act.wait_ge(s_r, order.find[("context", g - 2)].k + 1)
                    act.activation(ex[:, g % 2, 0:S], slot(g), ACT.Exp, bias=nmx[:, g:g + 1],
                                   accum_out=sml[:, g:g + 1]).then_inc(s_e, 1)
                    act.activation(ex[:, g % 2, S:NK1], sctx[:, head % 2, t], ACT.Exp, bias=nmx[:, g:g + 1],
                                   accum_out=smc[:, g:g + 1]).then_inc(s_e, 1)

                def raw_latents(g):
                    act.wait_ge(s_t, g + 1)
                    if g >= RAWS:
                        act.wait_ge(s_dlo, g - RAWS + 1)
                        act.wait_ge(s_plo, g - RAWS + 1)
                    elif g == 2:
                        act.wait_ge(s_bo, 1)
                    act.activation(raw[:, g % RAWS].rearrange("p k n -> p (k n)"),
                                   ps[:, 4:6, :].rearrange("p k n -> p (k n)"), ACT.Copy).then_inc(s_raw, 1)

                def evacuate(u):
                    act.wait_ge(s_r, u.k + 1)
                    bank = ps[:, u.bank, :]
                    if u.kind == "context":
                        g = u.at[0]
                        columns_free(act, g)
                        act.activation(pch[:, columns(g)], bank[0:SCP, 0:P], ACT.Copy).then_inc(s_pc, 1)
                    elif u.kind == "values":
                        if u.at[0]:
                            act.wait_ge(s_r, order.find[("project", u.at[0] - 1)].k + 1)
                        act.activation(oh[:], bank[:, 0:2 * P], ACT.Copy).then_inc(s_oh, 1)
                    elif u.kind == "stack":
                        head, n = u.at
                        if head >= 2:
                            act.wait_ge(s_s, (head - 1) * TQ)
                        if n < 4:
                            dst, src = qst[:, head % 2, n % 2, (n // 2) * BLK:(n // 2 + 1) * BLK], bank
                        elif n < 6:
                            dst, src = kst[:, head % 2, (n - 4) * BLK:(n - 3) * BLK], bank
                        else:
                            dst, src = kst[:, head % 2, S:NK1], bank[:, 0:SCP]
                        act.activation(dst, src, ACT.Copy).then_inc(s_act, 1)
                    elif u.kind == "scores":
                        head, n = u.at
                        if head >= 2:
                            act.wait_ge(s_nmc, head - 1)
                            act.wait_ge(s_e, 2 * TQ * (head - 1))
                        act.activation(sctx[:, head % 2, 4 * n:4 * n + 4].rearrange("p t n -> p (t n)"),
                                       bank[:, 0:4 * SCP], ACT.Copy).then_inc(s_act, 1)

                def upper_queries(head, n):
                    if head:
                        act.wait_ge(s_r, order.transposed(head - 1, range(4)))
                    ts = HALVES[n]
                    act.activation(qc[:, ts, 0].bitcast(FP32R), twice(qs[:, head, ts]), ACT.Copy)\
                        .then_inc(s_hi2, 1)

                def upper_keys(head):
                    if head:
                        act.wait_ge(s_r, order.transposed(head - 1, range(4, NSTK)))
                    for rows, ts in KEY_ROWS:
                        i = act.activation(kc[0:rows, ts, 0].bitcast(FP32R), kvs[0:rows, head, ts, 0:DH1],
                                           ACT.Copy)
                    i.then_inc(s_hi2, 1)

                def upper_values(head):
                    if head >= 2:
                        act.wait_ge(s_r, order.find[("values", 4 * (head - 2) + 3)].k + 1)
                    for rows, ts in KEY_ROWS:
                        i = act.activation(vst[0:rows, head % 2, ts, 0:DH1],
                                           kvs[0:rows, head, ts, DH1:2 * DH1], ACT.Copy)
                    i.then_inc(s_hi2, 1)

                upper_queries(0, 0)
                upper_queries(0, 1)
                upper_keys(0)
                upper_values(0)
                for u in order.uses[:order.first]:
                    evacuate(u)
                exps(0)
                raw_latents(0)
                upper_queries(1, 0)
                upper_queries(1, 1)
                exps(1)
                upper_keys(1)
                for g in range(NTQ + 2):
                    for u in order.step[g][:1]:
                        evacuate(u)
                    if g + 1 < NTQ:
                        raw_latents(g + 1)
                    for u in order.step[g][1:2]:
                        evacuate(u)
                    if g + 2 < NTQ:
                        exps(g + 2)
                    for u in order.step[g][2:]:
                        evacuate(u)
                    head, t = divmod(g, TQ)
                    if t == 1 and head + 1 < NH:
                        upper_values(head + 1)
                    if t in (3, 4) and head + 2 < NH:
                        upper_queries(head + 2, t - 3)
                    if t == 5 and head + 2 < NH:
                        upper_keys(head + 2)

            @block.vector
            def _(dve):
                def largest(g):
                    head, t = divmod(g, TQ)
                    if t == 0:
                        if head >= 2:
                            dve.wait_ge(s_mx, TQ * (head - 1))
                        dve.wait_ge(s_act, order.find[("scores", head, 1)].act)
                        dve.tensor_reduce(nmc[:, head % 2], sctx[:, head % 2], AX.X, ALU.max, negate=True)\
                            .then_inc(s_nmc, 1)
                    dve.wait_ge(s_s, g + 1)
                    dve.tensor_reduce(nml[:, g:g + 1], slot(g), AX.X, ALU.max, negate=True)\
                        .then_inc(s_nml, 1)
                    dve.wait_ge(s_nmc, head + 1)
                    dve.wait_ge(s_nml, g + 1)
                    dve.tensor_tensor(nmx[:, g:g + 1], nml[:, g:g + 1], nmc[:, head % 2, t:t + 1], ALU.min)\
                        .then_inc(s_mx, 1)

                def split_latents(g):
                    dve.wait_ge(s_raw, g + 1)
                    columns_free(dve, g)
                    dve.tensor_copy(pth[:, :, columns(g)], raw[:, g % RAWS]).then_inc(s_phi, 1)
                    pair = slice(g - 1, g + 1)
                    if g % 2:
                        dve.wait_ge(s_e, 2 * g + 2)
                        dve.tensor_tensor(sm[:, pair], sml[:, pair], smc[:, pair], ALU.add).then_inc(s_sm, 1)
                    dve.wait_ge(s_phi, g + 1)
                    dve.tensor_tensor(ptl[:, DVE_TILES, columns(g)], raw[:, g % RAWS, DVE_TILES],
                                      pth[:, DVE_TILES, columns(g)].bitcast(FP32), ALU.subtract)\
                        .then_inc(s_dlo, 1)
                    if g % 2:
                        dve.wait_ge(s_sm, g // 2 + 1)
                        dve.reciprocal(rc[:, pair], sm[:, pair]).then_inc(s_rc, 1)

                def evacuate(u):
                    bank = ps[:, u.bank, :]
                    if u.kind == "context":
                        g = u.at[0]
                        dve.wait_ge(s_pc, g + 1)
                        dve.tensor_tensor(pcl[:, columns(g)], bank[0:SCP, 0:P],
                                          pch[:, columns(g)].bitcast(FP32), ALU.subtract).then_inc(s_dve, 1)
                    elif u.kind == "values":
                        dve.wait_ge(s_oh, u.at[0] + 1)
                        dve.tensor_tensor(ol[:], bank[:, 0:2 * P], oh[:].bitcast(FP32), ALU.subtract)\
                            .then_inc(s_dve, 1)
                    elif u.kind == "project":
                        head, pair = divmod(u.at[0], TQ // 2)
                        t = HEADS1[head][0] * TQ + 2 * pair
                        dve.wait_ge(s_r, u.k + 1)
                        dve.wait_ge(s_rc, u.at[0] + 1)
                        for j in range(2):
                            g = 2 * u.at[0] + j
                            i = dve.scalar_tensor_tensor(m.x[:, t + j, :], bank[:, j * D:(j + 1) * D],
                                                         rc[:, g:g + 1], m.x[:, t + j, :], ALU.mult, ALU.add)
                        i.then_inc(s_dve, 1)

                dve.tensor_tensor(m.x[:], m.x[:], bo.unsqueeze(1).to_broadcast([P, NT, D]), ALU.add)\
                    .then_inc(s_bo, 1)
                largest(0)
                largest(1)
                dve.wait_ge(s_bo, 1)
                split_latents(0)
                for g in range(NTQ + 2):
                    if g + 2 < NTQ:
                        largest(g + 2)
                    for u in order.step[g]:
                        evacuate(u)
                    if g + 1 < NTQ:
                        split_latents(g + 1)

            @block.tensor
            def _(pe):
                def scores(g):
                    head, t = divmod(g, TQ)
                    if t == 0:
                        pe.wait_ge(s_act, order.stacked(head))
                    if g >= 2:
                        pe.wait_ge(s_e, 2 * (g - 2) + 1)
                    for w in range(2):
                        for n in range(2):
                            i = pe.matmul(slot(g)[:, n * BLK:(n + 1) * BLK],
                                          qst[:, head % 2, w, t * P:(t + 1) * P],
                                          kst[:, head % 2, n * BLK:(n + 1) * BLK], start=w == 0, stop=w == 1)
                    i.then_inc(s_s, 1)

                def transposes(g):
                    pe.wait_ge(s_e, 2 * g + 1)
                    if g:
                        pe.wait_ge(s_raw, g)
                    for kt in range(TQ):
                        i = pe.transpose(ps[:, 4 + kt // 4, (kt % 4) * P:(kt % 4 + 1) * P],
                                         ex[:, g % 2, kt * P:(kt + 1) * P], m.ident[:, :])
                    i.then_inc(s_t, 1)

                def fill(u):
                    order.wait_free(pe, u, s_act, s_dve)
                    if u.kind == "stack":
                        head, n = u.at
                        if n in (0, 2, 4, 6):
                            pe.wait_ge(s_cat, 3 * head + (n // 2 + 1 if n < 4 else 3))
                        if n < 4:
                            for j in range(4):
                                i = pe.transpose(ps[:, u.bank, j * P:(j + 1) * P],
                                                 qc[:, 4 * (n // 2) + j, n % 2].rearrange("p e d -> p (e d)"),
                                                 m.ident[:, :])
                        elif n < 6:
                            for j in range(4):
                                i = pe.transpose(ps[:, u.bank, j * P:(j + 1) * P],
                                                 kc[:, 4 * (n - 4) + j].rearrange("p e d -> p (e d)"),
                                                 m.ident[:, :])
                        else:
                            i = pe.transpose(ps[:, u.bank, 0:SCP],
                                             kc[0:SCP, TQ].rearrange("p e d -> p (e d)"), m.ident[0:SCP, 0:SCP])
                    elif u.kind == "scores":
                        head, n = u.at
                        b = HEADS1[head][0]
                        pe.wait_ge(s_act, order.stacked(head))
                        for j in range(4):
                            out = ps[:, u.bank, j * SCP:(j + 1) * SCP]
                            for w in range(2):
                                pe.matmul(out, qst[:, head % 2, w, (4 * n + j) * P:(4 * n + j + 1) * P],
                                          kst[:, head % 2, S:NK1], start=w == 0, stop=False)
                            i = pe.matmul(out, row0[:], maskm[:, b, :], start=False, stop=True)
                    elif u.kind == "context":
                        g = u.at[0]
                        pe.wait_ge(s_e, 2 * g + 2)
                        i = pe.transpose(ps[0:SCP, u.bank, 0:P], ex[:, g % 2, S:NK1], m.ident[:, :])
                    elif u.kind == "values":
                        q = u.at[0]
                        head, pair = divmod(q, TQ // 2)
                        c = slice((q % 2) * 2 * P, (q % 2 + 1) * 2 * P)
                        pe.wait_ge(s_dlo, 2 * q + 2)
                        pe.wait_ge(s_plo, 2 * q + 2)
                        pe.wait_ge(s_dve, order.find[("context", 2 * q + 1)].dve)
                        if pair == 0:
                            pe.wait_ge(s_vst, head + 1)
                        for kt in range(NKT):
                            for w in range(2):
                                if kt < TQ:
                                    mo = (pth, ptl)[w][:, kt, c]
                                    sta = vst[:, head % 2, kt, :]
                                else:
                                    mo = (pch, pcl)[w][:, c]
                                    sta = vst[0:SCP, head % 2, kt, :]
                                i = pe.matmul(ps[:, u.bank, 0:2 * P], sta, mo,
                                              start=kt == 0 and w == 0, stop=kt == NKT - 1 and w == 1)
                    else:
                        q = u.at[0]
                        h = HEADS1[q // (TQ // 2)][1]
                        pe.wait_ge(s_dve, order.find[("values", q)].dve)
                        for j in range(2):
                            for n, (st, mo) in enumerate(split_passes((oh, ol), (woh, wol))):
                                i = pe.matmul(ps[:, u.bank, j * D:(j + 1) * D], st[:, j * P:(j + 1) * P],
                                              mo[:, h, :], start=n == 0, stop=n == 2)
                    i.then_inc(s_r, 1)

                for u in order.uses[:order.first]:
                    fill(u)
                scores(0)
                scores(1)
                transposes(0)
                for g in range(NTQ + 2):
                    if g + 2 < NTQ:
                        scores(g + 2)
                    for u in order.step[g][:1]:
                        fill(u)
                    if g + 1 < NTQ:
                        transposes(g + 1)
                    for u in order.step[g][1:]:
                        fill(u)


def store_out(nc, m, a, out):
    with ExitStack() as ctx:
        s_out = ctx.enter_context(nc.semaphore("s_out"))
        with nc.Block() as block:
            @block.sync
            def _(sp):
                sp.dma_start(out.rearrange("b (t p) d -> p (b t) d", p=P), m.x[:]).then_inc(s_out, 16)
                sp.wait_ge(s_out, 16)


def program(nc, a, out):
    with ExitStack() as ctx:
        m = Memory(nc, ctx)
        raw0 = ctx.enter_context(nc.semaphore("f0_raw"))
        attention0(nc, m, a, raw0)
        m.norm.next(twice=True, affine=True)
        experts(nc, m, a, "f0", Layer(True, CH0, E // 2, [CH0, NMIX0]), raw0)
        m.norm.next(twice=False, affine=False)
        raw1 = ctx.enter_context(nc.semaphore("f1_raw"))
        attention1(nc, m, a, raw1)
        m.norm.next(twice=True, affine=True)
        experts(nc, m, a, "f1", Layer(False, CH1, E // 2 - 1, [CH1, CH1]), raw1)
        store_out(nc, m, a, out)


def kernel(**inputs):
    import numpy as np
    import concourse.bacc as bacc
    from concourse.bass_utils import run_bass_kernel_spmd

    v = {k: np.asarray(x) for k, x in inputs.items()}
    arrays = {}

    def parts(w, rows=P):
        return w.reshape(-1, rows, w.shape[-1]).transpose(1, 0, 2)

    def vec(g, rows=P):
        return g.reshape(-1, rows).T

    arrays["x"] = v["x"]
    arrays["ctx_768"] = v["ctx_768"]
    arrays["wqo0"] = np.stack([parts(v["L0_xattn_W_Q"]), parts(v["L0_xattn_W_O"])], 1)
    arrays["wkv0"] = np.stack([parts(v["L0_xattn_W_K"], HC), parts(v["L0_xattn_W_V"], HC)], 1)
    arrays["lat_gb"] = np.stack([vec(v["L0_xattn_ln_lat_g"]), vec(v["L0_xattn_ln_lat_b"])], 1)
    arrays["in_gb"] = np.stack([vec(v["L0_xattn_ln_in_g"], HC), vec(v["L0_xattn_ln_in_b"], HC)], 1)
    arrays["lx_gb"] = np.stack([vec(v["L1_xattn_ln_x_g"], HC), vec(v["L1_xattn_ln_x_b"], HC)], 1)
    arrays["c_ident"] = np.eye(P, dtype=np.float32)
    r = np.arange(NC0 * P)
    bd = (r[:, None] // SC == np.arange(D)[None, :] // DH0) & (r[:, None] < KC0)
    arrays["c_bd"] = bd.astype(np.float32).reshape(NC0, P, D).transpose(1, 0, 2)

    w1, w2 = (np.concatenate([v[f"L0_ffn_{n}"], v[f"L0_ffn_{s}"][None]]) for n, s in (("W1", "Ws1"), ("W2", "Ws2")))
    w3 = np.concatenate([v["L0_ffn_W3"], v["L0_ffn_Ws3"][None]]).transpose(0, 2, 1)
    full = CH0 * P

    def chunked_in(w, n):
        return w.reshape(-1, n, P, KD, P).transpose(0, 4, 1, 3, 2).reshape(-1, P, n, KD * P)

    def chunked_out(w, n):
        return w.reshape(-1, n, P, D).transpose(0, 2, 1, 3)

    def packed(ws, n):
        return np.concatenate([chunked_in(w, n) for w in ws[:-1]] + [chunked_out(ws[-1], n)], -1)\
            .reshape(-1, P, n * (len(ws) * 2 * P))

    arrays["f0_w"] = packed([w[:, :full] for w in (w1, w2, w3)], CH0)
    rests = []
    for w in (w1, w2, w3):
        r = w[:, full:].reshape(NMIX0, MIX0 * REM0, D)
        rests.append(np.concatenate([r, np.zeros((NMIX0, P - MIX0 * REM0, D), np.float32)], 1)
                     .reshape(1, NMIX0 * P, D))
    arrays["f0_wmix"] = packed(rests, NMIX0)[0]
    arrays["f0_wg"] = parts(v["L0_ffn_Wg"].T)
    arrays["f0_bias"] = v["L0_ffn_routing_bias"]
    j, e = np.arange(E)[None, :], np.arange(E)[:, None]
    arrays["c_tri"] = (j < e).astype(np.float32)
    arrays["wqkv1"] = parts(np.concatenate([v["L1_xattn_Wq"], v["L1_xattn_Wlkv"]]).T)
    arrays["wc1"] = parts(v["L1_xattn_Wkv"].T, HC)
    arrays["wo1"] = parts(v["L1_xattn_Wo"].T, DH1)
    arrays["ll_gb"] = np.stack([vec(v["L1_xattn_ln_l_g"]), vec(v["L1_xattn_ln_l_b"])], 1)
    arrays["qn_g"], arrays["kn_g"], arrays["bo"] = v["L1_xattn_qn_g"], v["L1_xattn_kn_g"], v["L1_xattn_bo"]
    arrays["mask"] = v["mask_BxS2_bk0"]
    arrays["f1_w"] = np.concatenate([
        packed([v["L1_ffn_W1"].transpose(0, 2, 1), v["L1_ffn_W2"]], CH1),
        v["L1_ffn_b1"].reshape(E, CH1, P).transpose(0, 2, 1)], -1)
    arrays["f1_wg"] = parts(v["L1_ffn_Wr"])
    arrays["f1_bias"] = v["L1_ffn_br"]
    arrays["f1_b2"] = v["L1_ffn_b2"]

    nc = bacc.Bacc("TRN2", target_bir_lowering=False, num_devices=1)
    arrays = {"in_" + k: np.ascontiguousarray(x) for k, x in arrays.items()}
    a = {k[3:]: nc.dram_tensor(k, x.shape, mybir.dt.from_np(x.dtype), kind="ExternalInput").ap()
         for k, x in arrays.items()}
    out = nc.dram_tensor("out_0", (B, S, D), FP32, kind="ExternalOutput").ap()
    program(nc, a, out)
    r = run_bass_kernel_spmd(nc, [arrays], core_ids=[0])
    return r.results[0]["out_0"]
```
